# Optimizing a Trainium2 kernel written in Bass

```python
import numpy as np
import jax
import jax.numpy as jnp

def _softmax(x, axis=-1):
    return jax.nn.softmax(x, axis=axis)

def _gelu(x):
    return jax.nn.gelu(x, approximate=True)

def _silu(x):
    return jax.nn.silu(x)

def _sigmoid(x):
    return jax.nn.sigmoid(x)

def _layernorm(x, axis=-1, eps=1e-05):
    m = jnp.mean(x, axis=axis, keepdims=True)
    v = jnp.var(x, axis=axis, keepdims=True)
    return (x - m) / jnp.sqrt(v + eps)

def _scatter_add(tgt, idx, src, axis=0):
    return tgt.at[idx].add(src)

def _segment_sum(src, seg, n):
    return jax.ops.segment_sum(src, seg, n)
kernel_name = 'mk_adj_ffn_d1_adj_r2_f66cbe'

def setup_inputs(seed: int=0):
    np.random.seed(seed)
    _w = jnp.asarray

    def _rec_inputs():
        import jax
        import jax.numpy as jnp
        _gk = jax.random.key(seed)
        x = -0.0005207 + 1.001 * jax.random.normal(jax.random.fold_in(_gk, 1), (4096, 128), jnp.float32)
        _a = jax.random.bernoulli(jax.random.fold_in(_gk, 2), 0.000976562, (4096, 4096))
        _a = jnp.logical_or(_a, jnp.swapaxes(_a, -1, -2))
        _a = jnp.logical_or(_a, jnp.eye(4096, dtype=bool))
        _af = _a.astype(jnp.float32)
        _af = _af * jax.random.uniform(jax.random.fold_in(_gk, 3), (4096, 4096), jnp.float32, 0.05, 1)
        adj = _af
        return (x, adj)
    x, adj = _rec_inputs()

    def _L0_gnn_setup():
        import jax, jax.numpy as jnp
        import numpy as np
        N = 4096
        D = 128
        L = 3

        def _cxin_conv(x, a, eps, W, b):
            ax = a @ x
            h = ax + (1.0 + eps[0]) * ax
            for i in range(L):
                h = jax.nn.relu(h @ W[i].T + b[i])
            return h
        key = jax.random.key(seed)
        ks = jax.random.split(key, 8)
        s = 1.0 / np.sqrt(D)
        return {'x1': jax.random.normal(ks[0], (N, D), jnp.float32), 'x2': jax.random.normal(ks[1], (N, D), jnp.float32), 'G1': jax.random.uniform(ks[2], (N, N), jnp.float32), 'G2': jax.random.uniform(ks[3], (N, N), jnp.float32), 'eps1': jnp.zeros((1,), jnp.float32), 'eps2': jnp.zeros((1,), jnp.float32), 'W1': jax.random.normal(ks[4], (L, D, D), jnp.float32) * s, 'b1': jnp.zeros((L, D), jnp.float32), 'W2': jax.random.normal(ks[5], (L, D, D), jnp.float32) * s, 'b2': jnp.zeros((L, D), jnp.float32), 'Wm': jax.random.normal(ks[6], (D, 2 * D), jnp.float32) * (1.0 / np.sqrt(2 * D)), 'bm': jnp.zeros((D,), jnp.float32)}
    _L0_gnn_all = _L0_gnn_setup()
    _L0_gnn_in = {k: v for k, v in _L0_gnn_all.items() if k in ('x2', 'eps1', 'eps2', 'W1', 'b1', 'W2', 'b2', 'Wm', 'bm')}
    del _L0_gnn_all

    def _L0_ffn_setup():
        import jax, jax.numpy as jnp
        import numpy as np
        B, A = (2048, 8)
        IN, OUT = (128, 128)
        SH1, SH2 = (128, 128)
        EH1, EH2 = (128, 64)
        E, TOPK = (4, 2)

        def _shared_mlp(x, W1, b1, W2, b2, W3, b3):
            h = jax.nn.relu(x @ W1 + b1)
            h = jax.nn.relu(h @ W2 + b2)
            return h @ W3 + b3

        def _experts_mlp(x, eW1, eb1, eW2, eb2, eW3, eb3):
            h = jax.nn.relu(jnp.einsum('baf,efh->ebah', x, eW1) + eb1[:, None, None, :])
            h = jax.nn.relu(jnp.einsum('ebah,ehg->ebag', h, eW2) + eb2[:, None, None, :])
            o = jnp.einsum('ebag,ego->ebao', h, eW3) + eb3[:, None, None, :]
            return jnp.moveaxis(o, 0, -1)
        key = jax.random.key(seed)
        ks = jax.random.split(key, 16)
        s = 0.05
        return {'x': jax.random.normal(ks[0], (B, A, IN), jnp.float32), 'sW1': jax.random.normal(ks[1], (IN, SH1), jnp.float32) * s, 'sb1': jnp.zeros((SH1,), jnp.float32), 'sW2': jax.random.normal(ks[2], (SH1, SH2), jnp.float32) * s, 'sb2': jnp.zeros((SH2,), jnp.float32), 'sW3': jax.random.normal(ks[3], (SH2, OUT), jnp.float32) * s, 'sb3': jnp.zeros((OUT,), jnp.float32), 'eW1': jax.random.normal(ks[4], (E, IN, EH1), jnp.float32) * s, 'eb1': jnp.zeros((E, EH1), jnp.float32), 'eW2': jax.random.normal(ks[5], (E, EH1, EH2), jnp.float32) * s, 'eb2': jnp.zeros((E, EH2), jnp.float32), 'eW3': jax.random.normal(ks[6], (E, EH2, OUT), jnp.float32) * s, 'eb3': jnp.zeros((E, OUT), jnp.float32), 'gW': jax.random.normal(ks[7], (IN, E), jnp.float32) * s, 'gb': jnp.zeros((E,), jnp.float32)}
    _L0_ffn_all = _L0_ffn_setup()
    _L0_ffn_in = {k: v for k, v in _L0_ffn_all.items() if k in ('sW1', 'sb1', 'sW2', 'sb2', 'sW3', 'sb3', 'eW1', 'eb1', 'eW2', 'eb2', 'eW3', 'eb3', 'gW', 'gb')}
    del _L0_ffn_all
    return {'x': x, 'adj': adj, 'L0_gnn_x2': _L0_gnn_in['x2'], 'L0_gnn_eps1': _L0_gnn_in['eps1'], 'L0_gnn_eps2': _L0_gnn_in['eps2'], 'L0_gnn_W1': _L0_gnn_in['W1'], 'L0_gnn_b1': _L0_gnn_in['b1'], 'L0_gnn_W2': _L0_gnn_in['W2'], 'L0_gnn_b2': _L0_gnn_in['b2'], 'L0_gnn_Wm': _L0_gnn_in['Wm'], 'L0_gnn_bm': _L0_gnn_in['bm'], 'L0_ffn_sW1': _L0_ffn_in['sW1'], 'L0_ffn_sb1': _L0_ffn_in['sb1'], 'L0_ffn_sW2': _L0_ffn_in['sW2'], 'L0_ffn_sb2': _L0_ffn_in['sb2'], 'L0_ffn_sW3': _L0_ffn_in['sW3'], 'L0_ffn_sb3': _L0_ffn_in['sb3'], 'L0_ffn_eW1': _L0_ffn_in['eW1'], 'L0_ffn_eb1': _L0_ffn_in['eb1'], 'L0_ffn_eW2': _L0_ffn_in['eW2'], 'L0_ffn_eb2': _L0_ffn_in['eb2'], 'L0_ffn_eW3': _L0_ffn_in['eW3'], 'L0_ffn_eb3': _L0_ffn_in['eb3'], 'L0_ffn_gW': _L0_ffn_in['gW'], 'L0_ffn_gb': _L0_ffn_in['gb']}

def reference(x, adj, L0_gnn_x2, L0_gnn_eps1, L0_gnn_eps2, L0_gnn_W1, L0_gnn_b1, L0_gnn_W2, L0_gnn_b2, L0_gnn_Wm, L0_gnn_bm, L0_ffn_sW1, L0_ffn_sb1, L0_ffn_sW2, L0_ffn_sb2, L0_ffn_sW3, L0_ffn_sb3, L0_ffn_eW1, L0_ffn_eb1, L0_ffn_eW2, L0_ffn_eb2, L0_ffn_eW3, L0_ffn_eb3, L0_ffn_gW, L0_ffn_gb):
    import jax
    import jax.numpy as jnp

    def _L0_gnn_ref(x1, x2, G1, G2, eps1, eps2, W1, b1, W2, b2, Wm, bm):
        import jax, jax.numpy as jnp
        import numpy as np
        N = 4096
        D = 128
        L = 3

        def _cxin_conv(x, a, eps, W, b):
            ax = a @ x
            h = ax + (1.0 + eps[0]) * ax
            for i in range(L):
                h = jax.nn.relu(h @ W[i].T + b[i])
            return h
        out1 = _cxin_conv(x1, G1, eps1, W1, b1)
        out2 = _cxin_conv(x2, G2, eps2, W2, b2)
        merged = jnp.concatenate((out1, out2), axis=1)
        return merged @ Wm.T + bm

    def _L0_ffn_ref(x, sW1, sb1, sW2, sb2, sW3, sb3, eW1, eb1, eW2, eb2, eW3, eb3, gW, gb):
        import jax, jax.numpy as jnp
        import numpy as np
        B, A = (2048, 8)
        IN, OUT = (128, 128)
        SH1, SH2 = (128, 128)
        EH1, EH2 = (128, 64)
        E, TOPK = (4, 2)

        def _shared_mlp(x, W1, b1, W2, b2, W3, b3):
            h = jax.nn.relu(x @ W1 + b1)
            h = jax.nn.relu(h @ W2 + b2)
            return h @ W3 + b3

        def _experts_mlp(x, eW1, eb1, eW2, eb2, eW3, eb3):
            h = jax.nn.relu(jnp.einsum('baf,efh->ebah', x, eW1) + eb1[:, None, None, :])
            h = jax.nn.relu(jnp.einsum('ebah,ehg->ebag', h, eW2) + eb2[:, None, None, :])
            o = jnp.einsum('ebag,ego->ebao', h, eW3) + eb3[:, None, None, :]
            return jnp.moveaxis(o, 0, -1)
        all_out = _experts_mlp(x, eW1, eb1, eW2, eb2, eW3, eb3)
        shared = _shared_mlp(x, sW1, sb1, sW2, sb2, sW3, sb3)
        gates = jax.nn.softmax(x @ gW + gb, axis=-1)
        topv, topi = jax.lax.top_k(gates, TOPK)
        topw = jax.nn.softmax(topv, axis=-1)
        sel = jnp.take_along_axis(all_out, topi[:, :, None, :], axis=-1)
        gated = jnp.sum(sel * topw[:, :, None, :], axis=-1)
        return shared + gated
    x = x + _L0_gnn_ref(_layernorm(x, axis=-1), L0_gnn_x2, adj, adj, L0_gnn_eps1, L0_gnn_eps2, L0_gnn_W1, L0_gnn_b1, L0_gnn_W2, L0_gnn_b2, L0_gnn_Wm, L0_gnn_bm)
    x = x + _L0_ffn_ref(_layernorm(x, axis=-1)[None], L0_ffn_sW1, L0_ffn_sb1, L0_ffn_sW2, L0_ffn_sb2, L0_ffn_sW3, L0_ffn_sb3, L0_ffn_eW1, L0_ffn_eb1, L0_ffn_eW2, L0_ffn_eb2, L0_ffn_eW3, L0_ffn_eb3, L0_ffn_gW, L0_ffn_gb)[0]
    return x

_drawn_inputs = setup_inputs


def setup_inputs(seed=0):
    import zlib

    import numpy as np

    out = dict(_drawn_inputs(seed))
    spreads = {'L0_gnn_b1': (0.0, 0.1),
     'L0_gnn_b2': (0.0, 0.1),
     'L0_gnn_bm': (0.0, 0.1),
     'L0_ffn_sb1': (0.0, 0.8),
     'L0_ffn_sb2': (0.0, 0.3),
     'L0_ffn_sb3': (0.0, 0.1),
     'L0_ffn_eb1': (0.0, 0.8),
     'L0_ffn_eb2': (0.0, 0.766),
     'L0_ffn_eb3': (0.0, 0.1),
     'L0_ffn_gb': (0.0, 0.676)}
    factors = {'L0_ffn_eW1': 3.219, 'L0_ffn_eW2': 2.84}
    for name, (base, spread) in spreads.items():
        noise = np.random.default_rng([zlib.crc32(name.encode()), seed]).standard_normal(out[name].shape)
        drawn = base * np.exp(spread * noise) if base else spread * noise
        out[name] = jnp.asarray(drawn.astype(out[name].dtype))
    for name, factor in factors.items():
        out[name] = (out[name] * factor).astype(out[name].dtype)
    return out
```

```python
from contextlib import ExitStack

import concourse.bass as bass
from concourse import mybir

F32 = mybir.dt.float32
F32R = mybir.dt.float32r
ALU = mybir.AluOpType
ACT = mybir.ActivationFunctionType
AX_X = mybir.AxisListType.X

P = 128
T = 4
ROWS = T * P
NEXP = 4
TOPK = 2
LAYERS = 3
CW = 2
RAW_RING = 8
SPLIT_RING = 4
PIECE_RING = 2
LN_EPS = 1e-5
WROWS = 3 * NEXP + 2

W_CONV = lambda v, layer: LAYERS * v + layer
W_MERGE = 2 * LAYERS
W_SHARED = W_MERGE + 2
W_EXP1 = W_SHARED + 3
W_EXP2 = W_EXP1 + NEXP
W_EXP3 = W_EXP2 + NEXP
W_GATE = W_EXP3 + NEXP // 2
W_COLS = W_GATE * P + NEXP

B_CONV = lambda v, layer: LAYERS * v + layer
B_SH = 2 * LAYERS
B_EXP1 = B_SH + 2
B_EXP2 = B_EXP1 + NEXP
B_COLS = B_EXP2 + NEXP // 2

C_ID = 0
C_SEL = P
C_LOWER = C_SEL + 2 * P
C_PART = C_LOWER + NEXP * NEXP
C_COLS = C_PART + 2

AT_CONV = (0, 2, 4)
AT_MERGE = 6
AT_TRANSPOSE = 8
AT_MLP1 = (9, 9, 10, 10, 11)
AT_MLP2 = (11, 12, 13)
AT_OUT = 14
LEAD = 2


def gnn_moe_kernel(nc, adj, x, x2, weights, bias_cols, bias_bc, bias_rows, consts, out):
    NB, NODES = adj.shape[0] // P, adj.shape[1] // ROWS
    CHUNKS = NODES // CW
    CCOLS = CW * ROWS
    XG = NODES // T
    WPIECES = -(-W_COLS // ROWS)
    pieces = sorted([(2 * g, "x2", g) for g in range(XG)]
                    + [(CHUNKS - 1 - 2 * k, "w", WPIECES - 1 - k) for k in range(WPIECES)])
    PIECES = len(pieces)
    x2_split = {g: i + 1 for i, (_, kind, g) in enumerate(pieces) if kind == "x2"}

    with ExitStack() as ctx:
        def sb(name, shape, dt=F32):
            return ctx.enter_context(nc.sbuf_tensor(name, shape, dt))

        def sem(name):
            return ctx.enter_context(nc.semaphore(name))

        xres = sb("xres", [P, NB, T, P])
        z_hi = sb("z_hi", [P, NODES, 2 * P], F32R)
        z_lo = sb("z_lo", [P, NODES, 2 * P], F32R)
        adj_raw = sb("adj_raw", [P, RAW_RING, CCOLS])
        adj_hi = sb("adj_hi", [P, SPLIT_RING, CCOLS], F32R)
        adj_lo = sb("adj_lo", [P, SPLIT_RING, CCOLS], F32R)
        w_hi = sb("w_hi", [P, W_COLS], F32R)
        w_lo = sb("w_lo", [P, W_COLS], F32R)
        act_hi = sb("act_hi", [P, 1 + NEXP, ROWS], F32R)
        act_lo = sb("act_lo", [P, 1 + NEXP, ROWS], F32R)
        work = sb("work", [P, 4, ROWS])
        ztmp = work[:, 2:4, :]
        ln_x1, x1 = work[:, 2, :], work[:, 3, :]
        lnx_hi = sb("lnx_hi", [P, ROWS], F32R)
        lnx_lo = sb("lnx_lo", [P, ROWS], F32R)
        wT = sb("wT", [WROWS, ROWS], F32R)
        cst = sb("cst", [P, C_COLS])
        sel = sb("sel", [WROWS, 2 * P], F32R)
        bcol = sb("bcol", [P, B_COLS])
        bbc = sb("bbc", [P, P + NEXP + 2])
        brow = sb("brow", [WROWS, P])
        brow_hi = sb("brow_hi", [WROWS, P], F32R)
        brow_lo = sb("brow_lo", [WROWS, P])
        brow_ext = sb("brow_ext", [WROWS, P], F32R)
        scale = sb("scale", [P, 2])
        stats = sb("stats", [P, 2, T, 6])
        mv = sb("mv", [P, 2, T, 2])
        var = sb("var", [P, 2, T])
        rstd = sb("rstd", [P, 2, T])
        mhalf = sb("mhalf", [P, T])
        eps = sb("eps", [P, T])
        waiter = sb("waiter", [P, 2])
        gl = sb("gl", [P, T, NEXP])
        gm = sb("gm", [P, 4, T])
        gd = sb("gd", [P, T, NEXP])
        ge = sb("ge", [P, T, NEXP])
        gates = sb("gates", [P, T, NEXP])
        beats = sb("beats", [P, T, NEXP, NEXP])
        ties = sb("ties", [P, T, NEXP, NEXP])
        rank = sb("rank", [P, T, NEXP])
        gw = sb("gw", [P, T, NEXP])
        gw_hi = sb("gw_hi", [P, T, NEXP], F32R)
        w_ext = sb("w_ext", [P, T, 16])

        banks = ctx.enter_context(nc.psum_tensor("banks", [P, 8, ROWS], F32))
        agg = [banks[:, v, :] for v in range(2)]
        conv_ps = [[banks[:, 2 + 2 * (s % 3) + v, :] for v in range(2)] for s in range(LAYERS)]
        merge_ps = banks[:, 2, :]
        lnT_ps = banks[:, 3, :]
        gate_ps = banks[:, 4, 0:T * NEXP]
        mlp_ps = [banks[:, k, :] for k in (5, 6, 7, 2, 3, 5, 6, 2)]
        wT_ps = banks[0:WROWS, 7, :]
        wbc_ps = [banks[:, 4, :], banks[:, 7, :]]
        out_ps = banks[:, 3, :]

        x_landed = [sem("x_landed_first"), sem("x_landed_rest")]
        adj_landed = [sem(f"adj_landed{k}") for k in range(RAW_RING)]
        piece_landed = [sem(f"piece_landed{k}") for k in range(PIECE_RING)]
        const_landed = sem("const_landed")
        out_stored = sem("out_stored")
        adj_hi_ready, adj_lo_ready, adj_used = sem("adj_hi_ready"), sem("adj_lo_ready"), sem("adj_used")
        z_hi_ready, z_lo_ready = sem("z_hi_ready"), sem("z_lo_ready")
        piece_hi, piece_lo = sem("piece_hi"), sem("piece_lo")
        ln_part, ln_stats, rstd_step, rstd_ready, ln_done = (
            sem("ln_part"), sem("ln_stats"), sem("rstd_step"), sem("rstd_ready"), sem("ln_done"))
        bm_added = sem("bm_added")
        setup_step, setup_done, mhalf_ready = sem("setup_step"), sem("setup_done"), sem("mhalf_ready")
        agg_half_done = sem("agg_half_done")
        conv_mm, conv_hi, conv_h, conv_lo = sem("conv_mm"), sem("conv_hi"), sem("conv_h"), sem("conv_lo")
        merge_mm, x1_ready = sem("merge_mm"), sem("x1_ready")
        lnT_mm, lnT_hi_ready, lnT_lo_ready = sem("lnT_mm"), sem("lnT_hi_ready"), sem("lnT_lo_ready")
        gate_mm, gate_step, gate_tie, gate_ready = sem("gate_mm"), sem("gate_step"), sem("gate_tie"), sem("gate_ready")
        wT_mm, wT_ready, wbc_mm = sem("wT_mm"), sem("wT_ready"), sem("wbc_mm")
        mlp_mm, mlp_hi, mlp_h, mlp_lo = sem("mlp_mm"), sem("mlp_hi"), sem("mlp_h"), sem("mlp_lo")
        pair_gated, pair_hi = sem("pair_gated"), sem("pair_hi")
        out_mm, out_ready = sem("out_mm"), sem("out_ready")

        x_rows = x.rearrange("(b p t) f -> p b (t f)", p=P, t=T)
        x2_rows = x2.rearrange("(b p t) f -> b p (t f)", p=P, t=T)
        out_rows = out.rearrange("(b p t) f -> b p (t f)", p=P, t=T)

        def wtile(w, k):
            return w[:, k * P:(k + 1) * P]

        def tile_cols(t):
            return slice(t * P, (t + 1) * P)

        def piece_cols(k):
            first = k * ROWS
            return first, min(W_COLS, first + ROWS)

        def block_rows(n):
            return xres[:, n].rearrange("p t f -> p (t f)")

        def node_group(g):
            return slice(T * g, T * g + T)

        def eb(ap):
            return ap.unsqueeze(2).to_broadcast([P, T, NEXP])

        block = ctx.enter_context(nc.Block())

        @block.sync
        def _(sp):
            def load_chunk(b, c):
                if not (isinstance(b, int) and CHUNKS * b + c < RAW_RING):
                    sp.wait_ge(adj_hi_ready, b * CHUNKS + (c + 1 - RAW_RING))
                    sp.wait_ge(adj_lo_ready, b * CHUNKS + (c + 1 - RAW_RING))
                row = b * P
                sp.dma_start(adj_raw[:, c % RAW_RING, :],
                             adj[bass.ds(row, P), c * CCOLS:(c + 1) * CCOLS]
                             ).then_inc(adj_landed[c % RAW_RING], 16)

            sp.dma_start(xres[:, 0].rearrange("p t f -> p (t f)"), x_rows[:, 0]).then_inc(x_landed[0], 16)
            load_chunk(0, 0)
            sp.dma_start(xres[:, 1:NB].rearrange("p b t f -> p b (t f)"),
                         x_rows[:, 1:NB]).then_inc(x_landed[1], 16)
            for c in range(1, 4):
                load_chunk(0, c)
            sp.dma_start(cst[:], consts).then_inc(const_landed, 16)
            sp.dma_start(bcol[:], bias_cols).then_inc(const_landed, 16)
            sp.dma_start(bbc[:], bias_bc.partition_broadcast(P)).then_inc(const_landed, 16)
            sp.dma_start(brow[:], bias_rows).then_inc(const_landed, 16)
            for c in range(4, CHUNKS):
                load_chunk(0, c)
            with sp.Fori(1, NB) as b:
                for c in range(CHUNKS):
                    load_chunk(b, c)
            with sp.Fori(0, NB) as n:
                sp.wait_ge(out_ready, n + 1)
                sp.dma_start(out_rows[n], block_rows(n)).then_inc(out_stored, 16)
            sp.wait_ge(out_stored, 16 * NB)

        @block.gpsimd
        def _(pool):
            nc.gpsimd.memset(eps[:], LN_EPS).then_inc(mhalf_ready, 1)
            nc.gpsimd.memset(mhalf[:], -0.5).then_inc(mhalf_ready, 1)
            pool.wait_ge(mhalf_ready, 2)

            def inverse_std(k, slot):
                pool.wait_ge(ln_stats, k + 1)
                nc.gpsimd.tensor_tensor(var[:, slot], mv[:, slot, :, 1], eps[:], ALU.add
                                        ).then_inc(rstd_step, 1)
                pool.wait_ge(rstd_step, k + 1)
                nc.gpsimd.tensor_tensor(rstd[:, slot], var[:, slot], mhalf[:], ALU.pow
                                        ).then_inc(rstd_ready, 1)

            for g in range(XG):
                inverse_std(g, g % 2)
                if g >= 1:
                    if g == 1:
                        pool.wait_ge(const_landed, 64)
                    pool.wait_ge(ln_done, g)
                    nc.gpsimd.tensor_tensor(xres[:, g - 1], xres[:, g - 1],
                                            bbc[:, 0:P].unsqueeze(1).to_broadcast([P, T, P]), ALU.add
                                            ).then_inc(bm_added, 1)
            pool.wait_ge(ln_done, XG)
            nc.gpsimd.tensor_tensor(xres[:, XG - 1], xres[:, XG - 1],
                                    bbc[:, 0:P].unsqueeze(1).to_broadcast([P, T, P]), ALU.add
                                    ).then_inc(bm_added, 1)
            with pool.Fori(0, NB) as n:
                inverse_std(n + XG, 0)

        @block.scalar
        def _(act):
            def load_piece(k):
                if k >= PIECE_RING:
                    act.wait_ge(piece_hi, k - PIECE_RING + 1)
                    act.wait_ge(piece_lo, k - PIECE_RING + 1)
                _, kind, part = pieces[k]
                if kind == "x2":
                    act.dma_start(work[:, k % PIECE_RING, :], x2_rows[part]).then_inc(piece_landed[k % PIECE_RING], 16)
                else:
                    lo, hi = piece_cols(part)
                    act.dma_start(work[:, k % PIECE_RING, 0:hi - lo], weights[:, lo:hi]
                                  ).then_inc(piece_landed[k % PIECE_RING], 16)

            def split_piece(k):
                act.wait_ge(piece_landed[k % PIECE_RING], 16 * (k // PIECE_RING + 1))
                _, kind, part = pieces[k]
                if kind == "x2":
                    nc.scalar.activation(z_hi[:, node_group(part), P:2 * P],
                                         work[:, k % PIECE_RING, :].rearrange("p (t f) -> p t f", t=T),
                                         ACT.Copy).then_inc(piece_hi, 1)
                else:
                    lo, hi = piece_cols(part)
                    nc.scalar.activation(w_hi[:, lo:hi], work[:, k % PIECE_RING, 0:hi - lo], ACT.Copy
                                         ).then_inc(piece_hi, 1)
                if 1 <= k and k + PIECE_RING - 1 < PIECES:
                    load_piece(k + PIECE_RING - 1)

            def split_chunk(b, c):
                use = c // RAW_RING + 1
                act.wait_ge(adj_landed[c % RAW_RING], b * (16 * CHUNKS // RAW_RING) + 16 * use)
                if not (isinstance(b, int) and CHUNKS * b + c < SPLIT_RING):
                    act.wait_ge(adj_used, b * CHUNKS + (c + 1 - SPLIT_RING))
                nc.scalar.activation(adj_hi[:, c % SPLIT_RING, :], adj_raw[:, c % RAW_RING, :], ACT.Copy
                                     ).then_inc(adj_hi_ready, 1)

            def split_z(g):
                act.wait_ge(ln_done, g + 1)
                nc.scalar.activation(z_hi[:, node_group(g), 0:P],
                                     ztmp[:, g % 2, :].rearrange("p (t f) -> p t f", t=T), ACT.Copy
                                     ).then_inc(z_hi_ready, 1)

            def aggregated(n):
                for v in range(2):
                    if v == 0:
                        act.wait_ge(agg_half_done, n + 1)
                    else:
                        act.wait_ge(adj_used, n * CHUNKS + CHUNKS)
                    nc.scalar.activation(act_hi[:, v, :], agg[v], ACT.Copy, scale=scale[:, v:v + 1]
                                         ).then_inc(conv_hi, 1)

            def conv_out(n, s):
                for v in range(2):
                    act.wait_ge(conv_mm, n * (2 * LAYERS) + (2 * s + v + 1))
                    nc.scalar.activation(act_hi[:, v, :], conv_ps[s][v], ACT.Relu,
                                         bias=bcol[:, B_CONV(v, s):B_CONV(v, s) + 1]).then_inc(conv_hi, 1)
                    nc.scalar.activation(work[:, v, :], conv_ps[s][v], ACT.Relu,
                                         bias=bcol[:, B_CONV(v, s):B_CONV(v, s) + 1]).then_inc(conv_h, 1)

            def lnT(n):
                act.wait_ge(lnT_mm, n + 1)
                nc.scalar.activation(lnx_hi[:], lnT_ps, ACT.Copy).then_inc(lnT_hi_ready, 1)

            def mlp_out(n, j):
                b = (B_SH if j == 0 else B_EXP1 + j - 1) if j <= NEXP else (B_SH + 1 if j == 5 else B_EXP2 + j - 6)
                bias = bcol[:, b:b + 1]
                act.wait_ge(mlp_mm, n * 8 + (j + 1))
                if j <= 5:
                    nc.scalar.activation(act_hi[:, j % 5, :], mlp_ps[j], ACT.Relu, bias=bias).then_inc(mlp_hi, 1)
                if j >= 3:
                    act.wait_ge(mlp_lo, n * 8 + (j - 2))
                nc.scalar.activation(work[:, j % 3, :], mlp_ps[j], ACT.Relu, bias=bias).then_inc(mlp_h, 1)

            def gate_exp(n, step, e_out):
                act.wait_ge(gate_step, n * GATE_STEPS + (step - 1))
                nc.scalar.activation(e_out, gd[:], ACT.Exp).then_inc(gate_step, 1)

            def gate_rows(n):
                act.wait_ge(wT_mm, n + 1)
                nc.scalar.activation(wT[:], wT_ps, ACT.Copy).then_inc(wT_ready, 1)

            def stages(n, c):
                if c == 1 - LEAD:
                    aggregated(n)
                for s in range(LAYERS):
                    if c == AT_CONV[s]:
                        conv_out(n, s)
                if c == AT_TRANSPOSE:
                    lnT(n)
                for j in range(8):
                    if c == (AT_MLP1 + AT_MLP2)[j]:
                        mlp_out(n, j)
                        if j == 0:
                            gate_exp(n, STEP_EXP1, ge[:])
                        if j == 2:
                            gate_exp(n, STEP_EXP2, ge[:])
                        if j == 5:
                            gate_rows(n)

            for k in range(PIECE_RING):
                load_piece(k)
            for c in range(CHUNKS):
                for k in range(PIECES):
                    if pieces[k][0] == c:
                        split_piece(k)
                split_chunk(0, c)
                if c % 2 == 0:
                    split_z(c // 2)
            act.wait_ge(const_landed, 64)
            nc.scalar.activation(sel[:], cst[0:WROWS, C_SEL:C_SEL + 2 * P], ACT.Copy).then_inc(setup_done, 1)
            act.wait_ge(setup_done, 3)
            with act.Fori(1, NB) as b:
                for c in range(CHUNKS):
                    split_chunk(b, c)
                    stages(b - 1, c - LEAD)
                for c in range(CHUNKS - LEAD, CHUNKS):
                    stages(b - 1, c)
            for c in range(1 - LEAD, CHUNKS):
                stages(NB - 1, c)

        @block.vector
        def _(dve):
            def split_piece(k):
                _, kind, part = pieces[k]
                src = work[:, k % PIECE_RING, :]
                dve.wait_ge(piece_hi, k + 1)
                if kind == "x2":
                    nc.vector.tensor_tensor(z_lo[:, node_group(part), P:2 * P],
                                            src.rearrange("p (t f) -> p t f", t=T),
                                            z_hi[:, node_group(part), P:2 * P].bitcast(F32), ALU.subtract
                                            ).then_inc(piece_lo, 1)
                else:
                    lo, hi = piece_cols(part)
                    nc.vector.tensor_tensor(w_lo[:, lo:hi], src[:, 0:hi - lo], w_hi[:, lo:hi].bitcast(F32),
                                            ALU.subtract).then_inc(piece_lo, 1)

            def split_chunk(b, c):
                dve.wait_ge(adj_hi_ready, b * CHUNKS + (c + 1))
                nc.vector.tensor_tensor(adj_lo[:, c % SPLIT_RING, :], adj_raw[:, c % RAW_RING, :],
                                        adj_hi[:, c % SPLIT_RING, :].bitcast(F32), ALU.subtract
                                        ).then_inc(adj_lo_ready, 1)

            def moments(k, slot, rows):
                for t in range(T):
                    nc.vector.bn_stats(stats[:, slot, t, :], rows[:, tile_cols(t)]).then_inc(ln_part, 1)
                dve.wait_ge(ln_part, k * T + T)
                nc.vector.tensor_copy(waiter[:, 0:1], stats[:, slot, T - 1, 0:1])
                for t in range(T):
                    last = nc.vector.bn_aggr(mv[:, slot, t, :], stats[:, slot, t, :])
                last.then_inc(ln_stats, 1)

            def normalise(k, slot, rows, dst):
                dve.wait_ge(rstd_ready, k + 1)
                for t in range(T):
                    last = nc.vector.tensor_scalar(dst[:, tile_cols(t)], rows[:, tile_cols(t)],
                                                   mv[:, slot, t, 0:1], rstd[:, slot, t:t + 1],
                                                   ALU.subtract, ALU.mult)
                last.then_inc(ln_done, 1)

            def split_z(g):
                dve.wait_ge(z_hi_ready, g + 1)
                nc.vector.tensor_tensor(z_lo[:, node_group(g), 0:P],
                                        ztmp[:, g % 2, :].rearrange("p (t f) -> p t f", t=T),
                                        z_hi[:, node_group(g), 0:P].bitcast(F32), ALU.subtract
                                        ).then_inc(z_lo_ready, 1)

            def aggregated(n):
                for v in range(2):
                    dve.wait_ge(conv_hi, n * 8 + (v + 1))
                    nc.vector.scalar_tensor_tensor(out=act_lo[:, v, :], in0=agg[v], scalar=scale[:, v:v + 1],
                                                   in1=act_hi[:, v, :].bitcast(F32), op0=ALU.mult,
                                                   op1=ALU.subtract).then_inc(conv_lo, 1)

            def conv_out(n, s):
                for v in range(2):
                    dve.wait_ge(conv_h, n * (2 * LAYERS) + (2 * s + v + 1))
                    nc.vector.tensor_tensor(act_lo[:, v, :], work[:, v, :], act_hi[:, v, :].bitcast(F32),
                                            ALU.subtract).then_inc(conv_lo, 1)

            def merged(n):
                dve.wait_ge(merge_mm, n + 1)
                dve.wait_ge(bm_added, XG)
                nc.vector.tensor_tensor(x1, merge_ps, block_rows(n), ALU.add).then_inc(x1_ready, 1)
                dve.wait_ge(x1_ready, n + 1)
                nc.vector.tensor_copy(waiter[:, 1:2], x1[:, 0:1])
                moments(n + XG, 0, x1)
                normalise(n + XG, 0, x1, ln_x1)

            def lnT(n):
                dve.wait_ge(lnT_hi_ready, n + 1)
                nc.vector.tensor_tensor(lnx_lo[:], lnT_ps, lnx_hi[:].bitcast(F32), ALU.subtract
                                        ).then_inc(lnT_lo_ready, 1)

            def mlp_out(n, j):
                h = work[:, j % 3, :]
                dve.wait_ge(mlp_h, n * 8 + (j + 1))
                if j <= 5:
                    slot = j % 5
                else:
                    q = j - 6
                    slot = 1 + 2 * q
                    dve.wait_ge(wbc_mm, n * 2 + (q + 1))
                    nc.vector.tensor_tensor(h, h, wbc_ps[q], ALU.mult).then_inc(pair_gated, 1)
                    dve.wait_ge(pair_gated, n * 2 + (q + 1))
                    nc.vector.tensor_copy(act_hi[:, slot, :], h).then_inc(pair_hi, 1)
                    dve.wait_ge(pair_hi, n * 2 + (q + 1))
                nc.vector.tensor_tensor(act_lo[:, slot, :], h, act_hi[:, slot, :].bitcast(F32), ALU.subtract
                                        ).then_inc(mlp_lo, 1)

            def gate_logits(n):
                base = n * GATE_STEPS
                dve.wait_ge(gate_mm, n + 1)
                nc.vector.tensor_tensor(gl[:], gate_ps.rearrange("p (t e) -> p t e", t=T),
                                        bbc[:, P:P + NEXP].unsqueeze(1).to_broadcast([P, T, NEXP]),
                                        ALU.add).then_inc(gate_step, 1)
                dve.wait_ge(gate_step, base + 1)
                nc.vector.tensor_reduce(gm[:, 0], gl[:], AX_X, ALU.max).then_inc(gate_step, 1)
                dve.wait_ge(gate_step, base + 2)
                nc.vector.tensor_tensor(gd[:], gl[:], eb(gm[:, 0]), ALU.subtract).then_inc(gate_step, 1)

            def gate_softmax(n):
                base = n * GATE_STEPS
                dve.wait_ge(gate_step, base + STEP_EXP1)
                nc.vector.tensor_reduce(gm[:, 1], ge[:], AX_X, ALU.add).then_inc(gate_step, 1)
                dve.wait_ge(gate_step, base + 5)
                nc.vector.reciprocal(gm[:, 2], gm[:, 1]).then_inc(gate_step, 1)
                dve.wait_ge(gate_step, base + 6)
                nc.vector.tensor_tensor(gates[:], ge[:], eb(gm[:, 2]), ALU.mult).then_inc(gate_step, 1)
                dve.wait_ge(gate_step, base + 7)
                nc.vector.tensor_reduce(gm[:, 3], gates[:], AX_X, ALU.max).then_inc(gate_step, 1)
                dve.wait_ge(gate_step, base + 8)
                nc.vector.tensor_tensor(gd[:], gates[:], eb(gm[:, 3]), ALU.subtract).then_inc(gate_step, 1)

            def gate_top2(n):
                base = n * GATE_STEPS
                mine = gates[:].unsqueeze(3).to_broadcast([P, T, NEXP, NEXP])
                other = gates[:].unsqueeze(2).to_broadcast([P, T, NEXP, NEXP])
                lower = cst[:, C_LOWER:C_LOWER + NEXP * NEXP].rearrange("p (e j) -> p e j", e=NEXP)
                nc.vector.tensor_tensor(ties[:], other, mine, ALU.is_equal).then_inc(gate_tie, 1)
                nc.vector.tensor_tensor(beats[:], other, mine, ALU.is_gt).then_inc(gate_tie, 1)
                dve.wait_ge(gate_tie, n * 5 + 2)
                nc.vector.tensor_tensor(ties[:], ties[:], lower.unsqueeze(1).to_broadcast([P, T, NEXP, NEXP]),
                                        ALU.mult).then_inc(gate_tie, 1)
                dve.wait_ge(gate_tie, n * 5 + 3)
                nc.vector.tensor_tensor(beats[:], beats[:], ties[:], ALU.add).then_inc(gate_tie, 1)
                dve.wait_ge(gate_tie, n * 5 + 4)
                nc.vector.tensor_reduce(rank[:], beats[:], AX_X, ALU.add).then_inc(gate_tie, 1)
                dve.wait_ge(gate_tie, n * 5 + 5)
                dve.wait_ge(gate_step, base + STEP_EXP2)
                nc.vector.scalar_tensor_tensor(out=gw[:], in0=rank[:], scalar=float(TOPK) - 0.5, in1=ge[:],
                                               op0=ALU.is_lt, op1=ALU.mult).then_inc(gate_step, 1)
                dve.wait_ge(gate_step, base + 11)
                nc.vector.tensor_reduce(gm[:, 1], gw[:], AX_X, ALU.add).then_inc(gate_step, 1)
                dve.wait_ge(gate_step, base + 12)
                nc.vector.reciprocal(gm[:, 2], gm[:, 1]).then_inc(gate_step, 1)
                dve.wait_ge(gate_step, base + 13)
                nc.vector.tensor_tensor(gw[:], gw[:], eb(gm[:, 2]), ALU.mult).then_inc(gate_step, 1)
                dve.wait_ge(gate_step, base + 14)
                nc.vector.tensor_copy(gw_hi[:], gw[:]).then_inc(gate_step, 1)
                dve.wait_ge(gate_step, base + 15)
                for k in range(2):
                    nc.vector.tensor_copy(w_ext[:, :, k * NEXP:(k + 1) * NEXP], gw_hi[:].bitcast(F32)
                                          ).then_inc(gate_ready, 1)
                nc.vector.tensor_tensor(w_ext[:, :, 2 * NEXP:3 * NEXP], gw[:], gw_hi[:].bitcast(F32),
                                        ALU.subtract).then_inc(gate_ready, 1)

            def result(n):
                dve.wait_ge(out_mm, n + 1)
                nc.vector.tensor_tensor(block_rows(n), out_ps, x1, ALU.add).then_inc(out_ready, 1)

            def stages(n, c):
                if c == 1 - LEAD:
                    aggregated(n)
                for s in range(LAYERS):
                    if c == AT_CONV[s]:
                        conv_out(n, s)
                if c == AT_MERGE:
                    merged(n)
                if c == AT_TRANSPOSE:
                    lnT(n)
                for j in range(8):
                    if c == (AT_MLP1 + AT_MLP2)[j]:
                        if j == 0:
                            gate_logits(n)
                        mlp_out(n, j)
                        if j == 1:
                            gate_softmax(n)
                        if j == 3:
                            gate_top2(n)
                if c == AT_OUT:
                    result(n)

            nc.vector.memset(w_ext[:], 1.0)
            dve.wait_ge(x_landed[0], 16)
            moments(0, 0, block_rows(0))
            dve.wait_ge(x_landed[1], 16)
            for c in range(CHUNKS):
                if c % 2 == 0:
                    g = c // 2
                    normalise(g, g % 2, block_rows(g), ztmp[:, g % 2, :])
                    split_z(g)
                for k in range(PIECES):
                    if pieces[k][0] == c:
                        split_piece(k)
                split_chunk(0, c)
                if c % 2 == 0 and g + 1 < XG:
                    moments(g + 1, (g + 1) % 2, block_rows(g + 1))
            dve.wait_ge(const_landed, 64)
            nc.vector.tensor_scalar(scale[:], bbc[:, P + NEXP:P + NEXP + 2], 1.0, 1.0, ALU.add, ALU.add
                                    ).then_inc(setup_done, 1)
            nc.vector.tensor_copy(brow_hi[:], brow[:]).then_inc(setup_step, 1)
            dve.wait_ge(setup_step, 1)
            nc.vector.tensor_tensor(brow_lo[:], brow[:], brow_hi[:].bitcast(F32), ALU.subtract
                                    ).then_inc(setup_step, 1)
            dve.wait_ge(setup_step, 2)
            nc.vector.tensor_scalar(brow_lo[:], brow_lo[:], cst[0:WROWS, C_PART + 1:C_PART + 2], None, ALU.mult
                                    ).then_inc(setup_step, 1)
            dve.wait_ge(setup_step, 3)
            nc.vector.scalar_tensor_tensor(out=brow_ext[:], in0=brow_hi[:].bitcast(F32),
                                           scalar=cst[0:WROWS, C_PART:C_PART + 1], in1=brow_lo[:],
                                           op0=ALU.mult, op1=ALU.add).then_inc(setup_done, 1)
            dve.wait_ge(setup_done, 3)
            with dve.Fori(1, NB) as b:
                for c in range(CHUNKS):
                    split_chunk(b, c)
                    stages(b - 1, c - LEAD)
                for c in range(CHUNKS - LEAD, CHUNKS):
                    stages(b - 1, c)
            for c in range(1 - LEAD, CHUNKS):
                stages(NB - 1, c)

        @block.tensor
        def _(pe):
            def hi_passes(ps, wh, wl, xh, start):
                nc.tensor.matmul(ps, wh, xh, start=start, stop=False)
                nc.tensor.matmul(ps, wl, xh, start=False, stop=False)

            def lo_pass(ps, wh, xl, stop):
                return nc.tensor.matmul(ps, wh, xl, start=False, stop=stop)

            def row_passes(ps, ah, al, wh, wl, start, stop):
                nc.tensor.matmul(ps, ah, wh, start=start, stop=False)
                nc.tensor.matmul(ps, ah, wl, start=False, stop=False)
                return nc.tensor.matmul(ps, al, wh, start=False, stop=stop)

            def aggregate(b, c):
                pe.wait_ge(adj_hi_ready, b * CHUNKS + (c + 1))
                pe.wait_ge(adj_lo_ready, b * CHUNKS + (c + 1))
                slot = c % SPLIT_RING
                for v in range(2):
                    if c == 0 and not isinstance(b, int):
                        pe.wait_ge(conv_lo, b * 8 + (v - 7))
                    for k in range(CW):
                        zh = z_hi[:, CW * c + k, v * P:(v + 1) * P]
                        zl = z_lo[:, CW * c + k, v * P:(v + 1) * P]
                        ah = adj_hi[:, slot, k * ROWS:(k + 1) * ROWS]
                        al = adj_lo[:, slot, k * ROWS:(k + 1) * ROWS]
                        last = c == CHUNKS - 1 and k == CW - 1
                        nc.tensor.matmul(agg[v], zh, ah, start=(c == 0 and k == 0), stop=False)
                        nc.tensor.matmul(agg[v], zl, ah, start=False, stop=False)
                        ins = nc.tensor.matmul(agg[v], zh, al, start=False, stop=last)
                    if c == CHUNKS - 1 and v == 0:
                        ins.then_inc(agg_half_done, 1)
                ins.then_inc(adj_used, 1)

            def conv_layer(n, s):
                for v in range(2):
                    k = W_CONV(v, s)
                    pe.wait_ge(conv_hi, n * 8 + (2 * s + v + 1))
                    hi_passes(conv_ps[s][v], wtile(w_hi, k), wtile(w_lo, k), act_hi[:, v, :], True)
                    pe.wait_ge(conv_lo, n * 8 + (2 * s + v + 1))
                    lo_pass(conv_ps[s][v], wtile(w_hi, k), act_lo[:, v, :], True).then_inc(conv_mm, 1)

            def merge(n):
                pe.wait_ge(conv_hi, n * 8 + 8)
                pe.wait_ge(conv_lo, n * 8 + 8)
                for t in range(T):
                    for v in range(2):
                        ins = row_passes(merge_ps[:, tile_cols(t)], act_hi[:, v, tile_cols(t)],
                                         act_lo[:, v, tile_cols(t)], wtile(w_hi, W_MERGE + v),
                                         wtile(w_lo, W_MERGE + v), v == 0, v == 1)
                ins.then_inc(merge_mm, 1)

            def transpose_ln(n):
                pe.wait_ge(ln_done, n + (XG + 1))
                for t in range(T):
                    ins = nc.tensor.transpose(lnT_ps[:, tile_cols(t)], ln_x1[:, tile_cols(t)],
                                              cst[:, C_ID:C_ID + P])
                ins.then_inc(lnT_mm, 1)

            def gate(n):
                pe.wait_ge(lnT_hi_ready, n + 1)
                pe.wait_ge(lnT_lo_ready, n + 1)
                cols = slice(W_GATE * P, W_GATE * P + NEXP)
                for t in range(T):
                    ins = row_passes(gate_ps[:, t * NEXP:(t + 1) * NEXP], lnx_hi[:, tile_cols(t)],
                                     lnx_lo[:, tile_cols(t)], w_hi[:, cols], w_lo[:, cols], True, True)
                ins.then_inc(gate_mm, 1)

            def mlp_layer(n, j):
                if j <= NEXP:
                    k = W_SHARED if j == 0 else W_EXP1 + j - 1
                    hi_passes(mlp_ps[j], wtile(w_hi, k), wtile(w_lo, k), lnx_hi[:], True)
                    lo_pass(mlp_ps[j], wtile(w_hi, k), lnx_lo[:], True).then_inc(mlp_mm, 1)
                    return
                parts = [(W_SHARED + 1, 0)] if j == 5 else [
                    (W_EXP2 + 2 * (j - 6) + i, 1 + 2 * (j - 6) + i) for i in range(2)]
                for i, (k, slot) in enumerate(parts):
                    pe.wait_ge(mlp_lo, n * 8 + (slot + 1))
                    hi_passes(mlp_ps[j], wtile(w_hi, k), wtile(w_lo, k), act_hi[:, slot, :], i == 0)
                    ins = lo_pass(mlp_ps[j], wtile(w_hi, k), act_lo[:, slot, :], i == len(parts) - 1)
                ins.then_inc(mlp_mm, 1)

            def gate_rows(n):
                pe.wait_ge(gate_ready, n * 3 + 3)
                for t in range(T):
                    ins = nc.tensor.transpose(wT_ps[:, tile_cols(t)], w_ext[:, t, 0:WROWS], cst[:, C_ID:C_ID + P])
                ins.then_inc(wT_mm, 1)

            def gate_spread(n):
                pe.wait_ge(wT_ready, n + 1)
                for q in range(2):
                    nc.tensor.matmul(wbc_ps[q], sel[:, tile_cols(q)], wT[:], start=True, stop=True
                                     ).then_inc(wbc_mm, 1)

            def output_layer(n):
                pe.wait_ge(mlp_lo, n * 8 + 8)
                for t in range(T):
                    nc.tensor.matmul(out_ps[:, tile_cols(t)], wT[:, tile_cols(t)], brow_ext[:], start=True,
                                     stop=False)
                    for k, slot in ((W_SHARED + 2, 0), (W_EXP3, 1), (W_EXP3 + 1, 3)):
                        ins = row_passes(out_ps[:, tile_cols(t)], act_hi[:, slot, tile_cols(t)],
                                         act_lo[:, slot, tile_cols(t)], wtile(w_hi, k), wtile(w_lo, k),
                                         False, slot == 3)
                ins.then_inc(out_mm, 1)

            def stages(n, c):
                for s in range(LAYERS):
                    if c == AT_CONV[s]:
                        if s == 0:
                            pe.wait_ge(piece_hi, PIECES)
                            pe.wait_ge(piece_lo, PIECES)
                            pe.wait_ge(setup_done, 3)
                        conv_layer(n, s)
                if c == AT_MERGE:
                    merge(n)
                if c == AT_TRANSPOSE:
                    transpose_ln(n)
                for j in range(8):
                    if c == (AT_MLP1 + AT_MLP2)[j]:
                        if j == 0:
                            gate(n)
                        mlp_layer(n, j)
                        if j == 5:
                            gate_rows(n)
                        if j == 6:
                            gate_spread(n)
                if c == AT_OUT:
                    output_layer(n)

            for c in range(CHUNKS):
                if c % 2 == 0:
                    pe.wait_ge(z_hi_ready, c // 2 + 1)
                    pe.wait_ge(z_lo_ready, c // 2 + 1)
                    pe.wait_ge(piece_lo, x2_split[c // 2])
                aggregate(0, c)
            with pe.Fori(1, NB) as b:
                for c in range(CHUNKS):
                    aggregate(b, c)
                    stages(b - 1, c)
            for c in range(CHUNKS):
                stages(NB - 1, c)


GATE_STEPS = 15
STEP_EXP1 = 4
STEP_EXP2 = 10


def _layout(a):
    import numpy as np

    n = a["adj"].shape[0]
    nb = n // ROWS
    adj = a["adj"].reshape(nb, P, T, nb, P, T).transpose(0, 4, 3, 5, 2, 1).reshape(nb * P, n * T)

    eW2 = a["L0_ffn_eW2"]
    pads = [np.concatenate([eW2[e], np.zeros_like(eW2[e])][::1 if e % 2 == 0 else -1], axis=1) for e in range(NEXP)]
    eW3 = a["L0_ffn_eW3"]
    weights = np.concatenate(
        [a["L0_gnn_W1"][k].T for k in range(LAYERS)] + [a["L0_gnn_W2"][k].T for k in range(LAYERS)]
        + [a["L0_gnn_Wm"][:, :P].T, a["L0_gnn_Wm"][:, P:].T]
        + [a["L0_ffn_sW1"], a["L0_ffn_sW2"], a["L0_ffn_sW3"]]
        + [a["L0_ffn_eW1"][e] for e in range(NEXP)] + pads
        + [eW3[2 * q:2 * q + 2].reshape(P, P) for q in range(NEXP // 2)] + [a["L0_ffn_gW"]], axis=1)
    bias_cols = np.concatenate([a["L0_gnn_b1"], a["L0_gnn_b2"], a["L0_ffn_sb1"][None], a["L0_ffn_sb2"][None],
                                a["L0_ffn_eb1"], a["L0_ffn_eb2"].reshape(NEXP // 2, P)]).T
    bias_bc = np.concatenate([a["L0_gnn_bm"], a["L0_ffn_gb"], a["L0_gnn_eps1"], a["L0_gnn_eps2"]])
    bias_rows = np.concatenate([a["L0_ffn_eb3"]] * 3 + [a["L0_ffn_sb3"][None]] * 2)

    consts = np.zeros((P, C_COLS), np.float32)
    consts[:, C_ID:C_ID + P] = np.eye(P)
    for e in range(NEXP):
        for row in (e, 2 * NEXP + e):
            consts[row, C_SEL + 64 * e:C_SEL + 64 * (e + 1)] = 1
    consts[:, C_LOWER:C_PART] = np.tril(np.ones((NEXP, NEXP)), -1).reshape(-1)
    hi_rows = np.array([1] * NEXP + [0] * NEXP + [1] * NEXP + [1, 0])
    consts[:WROWS, C_PART] = hi_rows
    consts[:WROWS, C_PART + 1] = 1 - hi_rows
    return {"adj": adj, "x": a["x"], "x2": a["L0_gnn_x2"], "weights": weights, "bias_cols": bias_cols,
            "bias_bc": bias_bc, "bias_rows": bias_rows, "consts": consts}


def kernel(**inputs):
    import numpy as _np
    import concourse.bacc as _bacc
    from concourse import mybir as _mybir
    from concourse.bass_utils import run_bass_kernel_spmd as _run

    nc = _bacc.Bacc("TRN2", target_bir_lowering=False, num_devices=1)
    arrays, args = {}, []
    for name, a in _layout({k: _np.asarray(v) for k, v in inputs.items()}).items():
        a = _np.ascontiguousarray(a)
        arrays[f"in_{name}_dram"] = a
        args.append(nc.dram_tensor(f"in_{name}_dram", a.shape, _mybir.dt.from_np(a.dtype), kind="ExternalInput").ap())
    args.append(nc.dram_tensor("out_0_dram", inputs["x"].shape, _mybir.dt.float32, kind="ExternalOutput").ap())
    gnn_moe_kernel(nc, *args)
    r = _run(nc, [arrays], core_ids=[0])
    return r.results[0]["out_0_dram"]
```

```python
from contextlib import ExitStack

import concourse.bass as bass
from concourse import mybir

F32 = mybir.dt.float32
F32R = mybir.dt.float32r
ALU = mybir.AluOpType
ACT = mybir.ActivationFunctionType
AX_X = mybir.AxisListType.X

P = 128
T = 4
ROWS = T * P
NEXP = 4
EH = 64
TOPK = 2
LAYERS = 3
CW = 2
RAW_RING = 8
SPLIT_RING = 4
PIECE_RING = 6
LN_EPS = 1e-5
WROWS = 3 * NEXP

W_MERGE = 2 * LAYERS
W_SHARED = W_MERGE + 2
W_EXP1 = W_SHARED + 3
W_EXP3 = W_EXP1 + NEXP
W_GATE = W_EXP3 + NEXP // 2
W_COLS = W_GATE * P + NEXP

B_SH = 2 * LAYERS
B_EXP1 = B_SH + 2
B_EXP2 = B_EXP1 + NEXP
B_MERGE = B_EXP2 + NEXP // 2
B_OUT = B_MERGE + 1
B_COLS = B_OUT + 1

C_ID = 0
C_SEL = P
C_LOWER = C_SEL + 2 * P
C_PART = C_LOWER + NEXP * NEXP
C_COLS = C_PART + 2

STAGES = (
    ("conv", 0, 0), ("conv", 1, 2), ("conv", 2, 4), ("merge", 0, 6), ("tokens", 0, 7),
    ("normalise", 0, 7), ("features", 0, 9), ("logits", 0, 10), ("gate", 0, 10),
    ("mlp", 0, 10), ("exp", 0, 10), ("mlp", 1, 10),
    ("softmax", 0, 10), ("exp", 1, 10), ("top2", 0, 10), ("mlp", 2, 11), ("mlp", 3, 11),
    ("mlp", 4, 11), ("rows", 0, 12), ("mlp", 5, 12), ("mlp", 6, 12), ("mlp", 7, 12),
    ("spread", 0, 12), ("out", 0, 14),
)
JOINED = ("gate", "exp", "softmax", "top2", "rows", "spread")
LEAD = 2
GATE_STEPS = 17


class Part:

    def __init__(self, n, half=None, joined=False):
        self.n, self.half, self.joined = n, half, joined
        self.tiles = range(T) if half is None else range(half * T // 2, (half + 1) * T // 2)
        self.cols = slice(self.tiles[0] * P, (self.tiles[-1] + 1) * P)
        self.ts = slice(self.tiles[0], self.tiles[-1] + 1)
        self.width = len(self.tiles)
        self.banks = (6, 7, 0, 1) if half == 1 else (2, 3, 4, 5)

    def count(self, per, before, k=0, size=1):
        if self.half is None:
            return self.n * per + (before + k + 1)
        return self.n * per + (2 * before + self.half * size + k + 1)

    def whole(self, per, before, k=0, size=1):
        return self.n * per + (before + k + 1)

    def both(self, per, before):
        return self.n * per + (2 * (before + 1) if self.joined else before + 1)


def parts_of(n, name):
    return [Part(n, joined=True)] if name in JOINED else [Part(n, 0), Part(n, 1)]


def gnn_moe_kernel(nc, adj, x, xT, x2, weights, w_exp2_in, bias_cols, bias_bc, bias_rows, consts, out):
    NB, NODES = adj.shape[0] // P, adj.shape[1] // ROWS
    CHUNKS = NODES // CW
    CCOLS = CW * ROWS
    XG = NODES // T
    WPIECES = -(-W_COLS // ROWS)
    pieces = sorted([(2 * g, k, g) for g in range(XG) for k in ("a x2", "b x")]
                    + [(CHUNKS - 1 - 2 * k, "c w", WPIECES - 1 - k) for k in range(WPIECES)])
    pieces = [(c, kind[2:], k) for c, kind, k in pieces]
    ends = lambda c: [(c, 0, None), (c + 1, 0, None), (c, 1, None), (c + 1, 1, c + 1)]
    PASSES = (ends(0)[:1] + [(1, 0, 0)] + ends(0)[2:]
              + [(c, v, (None, c)[v]) for c in range(2, CHUNKS - 2) for v in range(2)]
              + [(CHUNKS - 2, 0, CHUNKS - 2)] + ends(CHUNKS - 2)[1:])
    nth = {kind: [i for i, p in enumerate(pieces) if p[1] == kind] for kind in ("x", "x2", "w")}

    with ExitStack() as ctx:
        def sb(name, shape, dt=F32):
            return ctx.enter_context(nc.sbuf_tensor(name, shape, dt))

        def sem(name):
            return ctx.enter_context(nc.semaphore(name))

        z_hi = sb("z_hi", [P, NODES, 2 * P], F32R)
        z_lo = sb("z_lo", [P, NODES, 2 * P], F32R)
        adj_raw = sb("adj_raw", [P, RAW_RING, CCOLS])
        adj_hi = sb("adj_hi", [P, SPLIT_RING, CCOLS], F32R)
        adj_lo = sb("adj_lo", [P, SPLIT_RING, CCOLS], F32R)
        w_hi = sb("w_hi", [P, W_COLS], F32R)
        w_lo = sb("w_lo", [P, W_COLS], F32R)
        w_gate = sb("w_gate", [P, 2 * NEXP], F32R)
        w_exp2 = sb("w_exp2", [P, NEXP * EH])
        act_hi = sb("act_hi", [P, 4, ROWS], F32R)
        act_lo = sb("act_lo", [P, 4, ROWS], F32R)
        work = sb("work", [P, 9, ROWS])
        whole = [work[:, 4 + k, :] for k in range(3)]
        ztmp = work[:, 7:9, :]
        x1, ln_x1 = work[:, 7, :], work[:, 8, :]
        xres = sb("xres", [P, ROWS])
        y = sb("y", [P, ROWS])
        wT = sb("wT", [WROWS, ROWS], F32R)
        cst = sb("cst", [P, C_COLS])
        sel = sb("sel", [WROWS, 2 * P], F32R)
        bcol = sb("bcol", [P, B_COLS])
        bbc = sb("bbc", [P, NEXP + 2])
        brow = sb("brow", [WROWS, P])
        brow_hi = sb("brow_hi", [WROWS, P], F32R)
        brow_lo = sb("brow_lo", [WROWS, P])
        brow_ext = sb("brow_ext", [WROWS, P], F32R)
        scale = sb("scale", [P, 2])
        stats = sb("stats", [P, 2, T, 6])
        mv = sb("mv", [P, 2, T, 2])
        var = sb("var", [P, 2, T])
        rstd = sb("rstd", [P, 2, T])
        mhalf = sb("mhalf", [P, T])
        eps = sb("eps", [P, T])
        waiter = sb("waiter", [P, 2])
        warm = sb("warm", [P, 2])
        freed = sb("freed", [P, 1])
        gl = sb("gl", [P, T, NEXP])
        gm = sb("gm", [P, 4, T])
        gd = sb("gd", [P, T, NEXP])
        ge = sb("ge", [P, T, NEXP])
        gates = sb("gates", [P, T, NEXP])
        beats = sb("beats", [P, T, NEXP, NEXP])
        ties = sb("ties", [P, T, NEXP, NEXP])
        rank = sb("rank", [P, T, NEXP])
        gw = sb("gw", [P, T, NEXP])
        gw_hi = sb("gw_hi", [P, T, NEXP], F32R)
        w_ext = sb("w_ext", [P, T, WROWS])

        banks = ctx.enter_context(nc.psum_tensor("banks", [P, 8, ROWS], F32))
        agg = [banks[:, v, :] for v in range(2)]

        def ps(part, which):
            return banks[:, part.banks["ABCD".index(which)], part.cols]

        CONV_BANK = (("A", "B"), ("C", "D"), ("A", "B"))
        MERGE_BANK, TOKENS_BANK, FEATURES_BANK, GATE_BANK = "C", "D", "A", "B"
        MLP_BANK = "CDABCDAC"
        ROWS_BANK, SPREAD_BANK, OUT_BANK = "B", ("B", "D"), "A"

        def spread_ps(part, q):
            return banks[:, Part(part.n).banks["ABCD".index(SPREAD_BANK[q])], part.cols]

        def gate_ps(part):
            b = banks[:, part.banks["ABCD".index(GATE_BANK)], 0:T * 2 * NEXP]
            return b.rearrange("p (t k e) -> p t k e", t=T, k=2)[:, part.ts]

        adj_landed = [sem(f"adj_landed{k}") for k in range(RAW_RING)]
        piece_landed = [sem(f"piece_landed{k}") for k in range(PIECE_RING)]
        const_landed, xres_landed = sem("const_landed"), sem("xres_landed")
        y_free, stored, last_stored = sem("y_free"), sem("stored"), sem("last_stored")
        adj_hi_ready, adj_lo_ready, adj_used = sem("adj_hi_ready"), sem("adj_lo_ready"), sem("adj_used")
        z_hi_ready, z_lo_ready = sem("z_hi_ready"), sem("z_lo_ready")
        x2_hi, x2_lo, w_hi_ready, w_lo_ready = sem("x2_hi"), sem("x2_lo"), sem("w_hi_ready"), sem("w_lo_ready")
        ln_part, ln_stats, rstd_step, rstd_ready, ln_done = (
            sem("ln_part"), sem("ln_stats"), sem("rstd_step"), sem("rstd_ready"), sem("ln_done"))
        setup_step, setup_done, eps_ready, warm_ready = (
            sem("setup_step"), sem("setup_done"), sem("eps_ready"), sem("warm_ready"))
        agg_half_done, agg_hi, agg_lo = sem("agg_half_done"), sem("agg_hi"), sem("agg_lo")
        conv_mm, conv_hi, conv_lo = sem("conv_mm"), sem("conv_hi"), sem("conv_lo")
        conv_whole = [sem("conv_whole_act"), sem("conv_whole_dve")]
        merge_mm, x1_ready, tokens_mm = sem("merge_mm"), sem("x1_ready"), sem("tokens_mm")
        lnT_mm, lnT_hi, lnT_lo = sem("lnT_mm"), sem("lnT_hi"), sem("lnT_lo")
        logits_mm, logits_step, gate_step, gate_exp, gate_ready = (
            sem("logits_mm"), sem("logits_step"), sem("gate_step"), sem("gate_exp"), sem("gate_ready"))
        wT_mm, wT_ready, spread_mm = sem("wT_mm"), sem("wT_ready"), sem("spread_mm")
        mlp_mm, mlp_h = sem("mlp_mm"), sem("mlp_h")
        shared_hi, shared_lo = sem("shared_hi"), sem("shared_lo")
        pair_gated, pair_hi, pair_lo = sem("pair_gated"), sem("pair_hi"), sem("pair_lo")
        out_mm, out_ready = sem("out_mm"), sem("out_ready")

        x_rows = x.rearrange("(b p t) f -> b p (t f)", p=P, t=T)
        x2_rows = x2.rearrange("(b p t) f -> b p (t f)", p=P, t=T)

        def wtile(w, k):
            return w[:, k * P:(k + 1) * P]

        def tile_cols(t):
            return slice(t * P, (t + 1) * P)

        def weight_cols(k):
            return k * ROWS, min(W_COLS, (k + 1) * ROWS)

        def piece_source(i):
            _, kind, k = pieces[i]
            if kind == "w":
                return weights[:, slice(*weight_cols(k))]
            return (x_rows if kind == "x" else x2_rows)[k]

        def node_group(g):
            return slice(T * g, T * g + T)

        def by_tile(ap):
            return ap.rearrange("p (t f) -> p t f", f=P)

        def spread(ap, part):
            return ap[:, part.ts].unsqueeze(2).to_broadcast([P, part.width, NEXP])

        def peeled(b):
            return isinstance(b, int)

        block = ctx.enter_context(nc.Block())

        @block.sync
        def _(sp):
            def load_chunk(b, c):
                if not (peeled(b) and c < RAW_RING):
                    sp.wait_ge(adj_hi_ready, b * CHUNKS + (c + 1 - RAW_RING))
                    sp.wait_ge(adj_lo_ready, b * CHUNKS + (c + 1 - RAW_RING))
                sp.dma_start(adj_raw[:, c % RAW_RING, :],
                             adj[bass.ds(b * P, P), c * CCOLS:(c + 1) * CCOLS]
                             ).then_inc(adj_landed[c % RAW_RING], 16)

            def load_xres(n):
                sp.wait_ge(agg_lo, n * 2 + 1)
                sp.dma_start(xres[:], xT[:, bass.ds(n * ROWS, ROWS)]).then_inc(xres_landed, 16)

            for i in range(PIECE_RING):
                sp.dma_start(work[:, i, :], piece_source(i)).then_inc(piece_landed[i], 16)
                if i % 2 == 0:
                    load_chunk(0, i // 2)
            load_chunk(0, 3)
            sp.dma_start(cst[:], consts).then_inc(const_landed, 16)
            sp.dma_start(bcol[:], bias_cols).then_inc(const_landed, 16)
            sp.dma_start(bbc[:], bias_bc.partition_broadcast(P)).then_inc(const_landed, 16)
            sp.dma_start(brow[:], bias_rows).then_inc(const_landed, 16)
            sp.dma_start(w_exp2[:], w_exp2_in).then_inc(const_landed, 16)
            for c in range(4, CHUNKS):
                load_chunk(0, c)
            with sp.Fori(1, NB) as b:
                for c in range(CHUNKS):
                    load_chunk(b, c)
                    if c == RAW_RING + 1:
                        load_xres(b - 1)
            load_xres(NB - 1)
            for half in range(2):
                part = Part(NB - 1, half)
                sp.wait_ge(out_ready, part.count(1, 0))
                sp.dma_start(out[:, (NB - 1) * ROWS + part.cols.start:(NB - 1) * ROWS + part.cols.stop],
                             y[:, part.cols]).then_inc(last_stored, 16)
            sp.wait_ge(last_stored, 32)

        @block.gpsimd
        def _(pool):
            nc.gpsimd.memset(eps[:], LN_EPS).then_inc(y_free, 1)
            nc.gpsimd.memset(mhalf[:], -0.5).then_inc(eps_ready, 1)
            pool.wait_ge(y_free, 1)
            pool.wait_ge(eps_ready, 1)

            def inverse_std(k, slot, ts):
                pool.wait_ge(ln_stats, k)
                nc.gpsimd.tensor_tensor(var[:, slot, ts], mv[:, slot, ts, 1], eps[:, ts], ALU.add
                                        ).then_inc(rstd_step, 1)
                pool.wait_ge(rstd_step, k)
                nc.gpsimd.tensor_tensor(rstd[:, slot, ts], var[:, slot, ts], mhalf[:, ts], ALU.pow
                                        ).then_inc(rstd_ready, 1)

            for g in range(XG):
                inverse_std(g + 1, g % 2, slice(0, T))
                for i in nth["w"]:
                    if pieces[i][0] in (2 * g, 2 * g + 1):
                        lo, hi = weight_cols(pieces[i][2])
                        pool.wait_ge(w_hi_ready, pieces[i][2] + 1)
                        nc.gpsimd.tensor_tensor(w_lo[:, lo:hi], work[:, i % PIECE_RING, 0:hi - lo],
                                                w_hi[:, lo:hi].bitcast(F32), ALU.subtract
                                                ).then_inc(w_lo_ready, 1)
            with pool.Fori(0, NB - 1) as n:
                inverse_std(n + (XG + 1), 0, slice(0, T))
                pool.wait_ge(out_ready, n + 1)
                pool.dma_start(out[:, bass.ds(n * ROWS, ROWS)], y[:]).then_inc(stored, 16)
                pool.wait_ge(stored, n * 16 + 16)
                nc.gpsimd.tensor_tensor(freed[:], eps[:, 0:1], eps[:, 0:1], ALU.add).then_inc(y_free, 1)
            for half in range(2):
                part = Part(NB - 1, half)
                inverse_std(part.count(1, 0) + XG, 0, part.ts)

        @block.scalar
        def _(act):
            def load_piece(i):
                _, old, k = pieces[i - PIECE_RING]
                act.wait_ge({"x": ln_done, "x2": x2_lo, "w": w_lo_ready}[old], k + 1)
                if old != "x":
                    act.wait_ge({"x2": x2_hi, "w": w_hi_ready}[old], k + 1)
                src = piece_source(i)
                act.dma_start(work[:, i % PIECE_RING, 0:src.shape[1]], src).then_inc(piece_landed[i % PIECE_RING], 16)

            def split_piece(i):
                _, kind, k = pieces[i]
                act.wait_ge(piece_landed[i % PIECE_RING], 16 * (i // PIECE_RING + 1))
                if kind == "x2":
                    nc.scalar.activation(z_hi[:, node_group(k), P:2 * P], by_tile(work[:, i % PIECE_RING, :]),
                                         ACT.Copy).then_inc(x2_hi, 1)
                else:
                    lo, hi = weight_cols(k)
                    nc.scalar.activation(w_hi[:, lo:hi], work[:, i % PIECE_RING, 0:hi - lo], ACT.Copy
                                         ).then_inc(w_hi_ready, 1)

            def split_chunk(b, c):
                act.wait_ge(adj_landed[c % RAW_RING], b * (16 * CHUNKS // RAW_RING) + 16 * (c // RAW_RING + 1))
                if not (peeled(b) and c < SPLIT_RING):
                    act.wait_ge(adj_used, b * CHUNKS + (c + 1 - SPLIT_RING))
                nc.scalar.activation(adj_hi[:, c % SPLIT_RING, :], adj_raw[:, c % RAW_RING, :], ACT.Copy
                                     ).then_inc(adj_hi_ready, 1)

            def split_z(g):
                act.wait_ge(ln_done, g + 1)
                nc.scalar.activation(z_hi[:, node_group(g), 0:P], by_tile(ztmp[:, g % 2, :]), ACT.Copy
                                     ).then_inc(z_hi_ready, 1)

            def aggregated(n):
                for v in range(2):
                    if v == 0:
                        act.wait_ge(agg_half_done, n + 1)
                    else:
                        act.wait_ge(adj_used, n * CHUNKS + CHUNKS)
                    nc.scalar.activation(act_hi[:, v, :], agg[v], ACT.Copy, scale=scale[:, v:v + 1]
                                         ).then_inc(agg_hi, 1)

            def conv(part, s):
                for v in range(2):
                    bias = bcol[:, LAYERS * v + s:LAYERS * v + s + 1]
                    act.wait_ge(conv_mm, part.count(6, 2 * s, v, 2))
                    nc.scalar.activation(act_hi[:, v, part.cols], ps(part, CONV_BANK[s][v]), ACT.Relu,
                                         bias=bias).then_inc(conv_hi, 1)
                    if v == 0:
                        nc.scalar.activation(whole[0][:, part.cols], ps(part, CONV_BANK[s][0]), ACT.Relu,
                                             bias=bias).then_inc(conv_whole[0], 1)

            def features(part):
                act.wait_ge(lnT_mm, part.count(1, 0))
                nc.scalar.activation(act_hi[:, 3, part.cols], ps(part, FEATURES_BANK), ACT.Copy).then_inc(lnT_hi, 1)

            def mlp(part, j):
                b = (B_SH, B_EXP1, B_EXP1 + 1, B_EXP1 + 2, B_EXP1 + 3, B_SH + 1, B_EXP2, B_EXP2 + 1)[j]
                dst = (whole[0], work[:, 0, :], work[:, 1, :], work[:, 2, :], work[:, 3, :], whole[0],
                       whole[1], whole[2])[j]
                act.wait_ge(mlp_mm, part.count(8, j))
                if j in (0, 5):
                    nc.scalar.activation(act_hi[:, 0, part.cols], ps(part, MLP_BANK[j]), ACT.Relu,
                                         bias=bcol[:, b:b + 1]).then_inc(shared_hi, 1)
                nc.scalar.activation(dst[:, part.cols], ps(part, MLP_BANK[j]), ACT.Relu,
                                     bias=bcol[:, b:b + 1]).then_inc(mlp_h, 1)

            def exponential(part, which):
                act.wait_ge(gate_step, part.whole(GATE_STEPS, 1 if which == 0 else 6))
                nc.scalar.activation(ge[:, part.ts], gd[:, part.ts], ACT.Exp).then_inc(gate_exp, 1)

            def rows(part):
                act.wait_ge(wT_mm, part.whole(1, 0))
                nc.scalar.activation(wT[:, part.cols], ps(part, ROWS_BANK)[0:WROWS], ACT.Copy).then_inc(wT_ready, 1)

            def stage(part, name, k):
                if name == "conv":
                    conv(part, k)
                if name == "features":
                    features(part)
                if name == "mlp":
                    mlp(part, k)
                if name == "exp":
                    exponential(part, k)
                if name == "rows":
                    rows(part)

            act.wait_ge(warm_ready, 1)
            nc.scalar.activation(warm[:, 0:1], warm[:, 1:2], ACT.Exp)
            loaded = PIECE_RING
            for c in range(CHUNKS):
                for i in nth["x2"] + nth["w"]:
                    if pieces[i][0] == c:
                        split_piece(i)
                split_chunk(0, c)
                if c % 2 == 1:
                    split_z(c // 2)
                while loaded < len(pieces) and pieces[loaded - PIECE_RING][0] < c:
                    load_piece(loaded)
                    loaded += 1
            act.wait_ge(const_landed, 80)
            nc.scalar.activation(sel[:], cst[0:WROWS, C_SEL:C_SEL + 2 * P], ACT.Copy).then_inc(setup_done, 1)
            act.wait_ge(w_hi_ready, WPIECES)
            nc.scalar.activation(w_gate[:, 0:NEXP], w_hi[:, W_GATE * P:W_COLS].bitcast(F32), ACT.Copy
                                 ).then_inc(setup_done, 1)
            act.wait_ge(w_lo_ready, WPIECES)
            nc.scalar.activation(w_gate[:, NEXP:2 * NEXP], w_lo[:, W_GATE * P:W_COLS].bitcast(F32), ACT.Copy
                                 ).then_inc(setup_done, 1)
            act.wait_ge(setup_done, 5)
            with act.Fori(1, NB) as b:
                for c in range(CHUNKS + LEAD):
                    if c < CHUNKS:
                        split_chunk(b, c)
                    if c == LEAD - 1:
                        aggregated(b - 1)
                    for name, k, at in STAGES:
                        if at == c - LEAD:
                            stage(Part(b - 1), name, k)
            aggregated(NB - 1)
            for name, k, _ in STAGES:
                for part in parts_of(NB - 1, name):
                    stage(part, name, k)

        @block.vector
        def _(dve):
            def split_x2(g):
                i = nth["x2"][g]
                dve.wait_ge(x2_hi, g + 1)
                nc.vector.tensor_tensor(z_lo[:, node_group(g), P:2 * P], by_tile(work[:, i % PIECE_RING, :]),
                                        z_hi[:, node_group(g), P:2 * P].bitcast(F32), ALU.subtract
                                        ).then_inc(x2_lo, 1)

            def split_chunk(b, c):
                dve.wait_ge(adj_hi_ready, b * CHUNKS + (c + 1))
                nc.vector.tensor_tensor(adj_lo[:, c % SPLIT_RING, :], adj_raw[:, c % RAW_RING, :],
                                        adj_hi[:, c % SPLIT_RING, :].bitcast(F32), ALU.subtract
                                        ).then_inc(adj_lo_ready, 1)

            def moments(k, slot, src, tiles):
                for t in tiles:
                    last = nc.vector.bn_stats(stats[:, slot, t, :], src[:, tile_cols(t)])
                last.then_inc(ln_part, 1)
                dve.wait_ge(ln_part, k)
                nc.vector.tensor_copy(waiter[:, 0:1], stats[:, slot, tiles[-1], 0:1])
                for t in tiles:
                    last = nc.vector.bn_aggr(mv[:, slot, t, :], stats[:, slot, t, :])
                last.then_inc(ln_stats, 1)

            def normalise(k, slot, src, dst, tiles):
                dve.wait_ge(rstd_ready, k)
                for t in tiles:
                    last = nc.vector.tensor_scalar(dst[:, tile_cols(t)], src[:, tile_cols(t)],
                                                   mv[:, slot, t, 0:1], rstd[:, slot, t:t + 1],
                                                   ALU.subtract, ALU.mult)
                last.then_inc(ln_done, 1)

            def moments_x(g):
                i = nth["x"][g]
                dve.wait_ge(piece_landed[i % PIECE_RING], 16 * (i // PIECE_RING + 1))
                moments(g + 1, g % 2, work[:, i % PIECE_RING, :], range(T))

            def split_z(g):
                dve.wait_ge(z_hi_ready, g + 1)
                nc.vector.tensor_tensor(z_lo[:, node_group(g), 0:P], by_tile(ztmp[:, g % 2, :]),
                                        z_hi[:, node_group(g), 0:P].bitcast(F32), ALU.subtract
                                        ).then_inc(z_lo_ready, 1)

            def aggregated(n):
                for v in range(2):
                    dve.wait_ge(agg_hi, n * 2 + (v + 1))
                    nc.vector.scalar_tensor_tensor(out=act_lo[:, v, :], in0=agg[v], scalar=scale[:, v:v + 1],
                                                   in1=act_hi[:, v, :].bitcast(F32), op0=ALU.mult,
                                                   op1=ALU.subtract).then_inc(agg_lo, 1)

            def conv(part, s):
                for v in range(2):
                    if v == 0:
                        dve.wait_ge(conv_whole[0], part.count(3, s))
                    else:
                        dve.wait_ge(conv_hi, part.count(6, 2 * s, 1, 2))
                        nc.vector.tensor_scalar(whole[1][:, part.cols], ps(part, CONV_BANK[s][1]),
                                                bcol[:, LAYERS + s:LAYERS + s + 1], 0.0, ALU.add, ALU.max
                                                ).then_inc(conv_whole[1], 1)
                        dve.wait_ge(conv_whole[1], part.count(3, s))
                    nc.vector.tensor_tensor(act_lo[:, v, part.cols], whole[v][:, part.cols],
                                            act_hi[:, v, part.cols].bitcast(F32), ALU.subtract
                                            ).then_inc(conv_lo, 1)

            def merge(part):
                dve.wait_ge(merge_mm, part.count(1, 0))
                dve.wait_ge(xres_landed, part.n * 16 + 16)
                nc.vector.scalar_tensor_tensor(out=x1[:, part.cols], in0=ps(part, MERGE_BANK),
                                               scalar=bcol[:, B_MERGE:B_MERGE + 1], in1=xres[:, part.cols],
                                               op0=ALU.add, op1=ALU.add).then_inc(x1_ready, 1)

            def tokens(part):
                bank = banks[:, part.banks["ABCD".index(TOKENS_BANK)], :]
                dve.wait_ge(tokens_mm, part.count(1, 0))
                nc.vector.tensor_copy(waiter[:, 1:2], bank[:, part.cols.start:part.cols.start + 1])
                moments(part.count(1, 0) + XG, 0, bank, part.tiles)

            def normalise_x1(part):
                bank = banks[:, part.banks["ABCD".index(TOKENS_BANK)], :]
                normalise(part.count(1, 0) + XG, 0, bank, ln_x1, part.tiles)

            def features(part):
                dve.wait_ge(lnT_hi, part.count(1, 0))
                nc.vector.tensor_tensor(act_lo[:, 3, part.cols], ps(part, FEATURES_BANK),
                                        act_hi[:, 3, part.cols].bitcast(F32), ALU.subtract).then_inc(lnT_lo, 1)

            def mlp(part, j):
                if 1 <= j <= NEXP:
                    return
                dve.wait_ge(mlp_h, part.count(8, j))
                if j in (0, 5):
                    src, slot, signal = whole[0][:, part.cols], 0, shared_lo
                else:
                    q = j - 6
                    src, slot, signal = whole[1 + q][:, part.cols], 1 + q, pair_lo
                    dve.wait_ge(spread_mm, part.whole(2, q))
                    nc.vector.tensor_tensor(src, src, spread_ps(part, q), ALU.mult).then_inc(pair_gated, 1)
                    dve.wait_ge(pair_gated, part.count(2, q))
                    nc.vector.tensor_copy(act_hi[:, slot, part.cols], src).then_inc(pair_hi, 1)
                    dve.wait_ge(pair_hi, part.count(2, q))
                nc.vector.tensor_tensor(act_lo[:, slot, part.cols], src, act_hi[:, slot, part.cols].bitcast(F32),
                                        ALU.subtract).then_inc(signal, 1)

            def logits(part):
                ts = part.ts
                dve.wait_ge(logits_mm, part.count(1, 0))
                nc.vector.tensor_tensor(gl[:, ts], gate_ps(part)[:, :, 0],
                                        bbc[:, 0:NEXP].unsqueeze(1).to_broadcast([P, part.width, NEXP]),
                                        ALU.add).then_inc(logits_step, 1)
                dve.wait_ge(logits_step, part.count(2, 0, 0, 2))
                nc.vector.tensor_tensor(gl[:, ts], gate_ps(part)[:, :, 1], gl[:, ts], ALU.add
                                        ).then_inc(logits_step, 1)

            def gate(part):
                ts = part.ts
                dve.wait_ge(logits_step, part.both(2, 1))
                nc.vector.tensor_reduce(gm[:, 0, ts], gl[:, ts], AX_X, ALU.max).then_inc(gate_step, 1)
                dve.wait_ge(gate_step, part.whole(GATE_STEPS, 0))
                nc.vector.tensor_tensor(gd[:, ts], gl[:, ts], spread(gm[:, 0], part), ALU.subtract
                                        ).then_inc(gate_step, 1)

            def softmax(part):
                ts = part.ts
                step = lambda k: part.whole(GATE_STEPS, 1 + k)
                dve.wait_ge(gate_exp, part.whole(2, 0))
                nc.vector.tensor_reduce(gm[:, 1, ts], ge[:, ts], AX_X, ALU.add).then_inc(gate_step, 1)
                dve.wait_ge(gate_step, step(1))
                nc.vector.reciprocal(gm[:, 2, ts], gm[:, 1, ts]).then_inc(gate_step, 1)
                dve.wait_ge(gate_step, step(2))
                nc.vector.tensor_tensor(gates[:, ts], ge[:, ts], spread(gm[:, 2], part), ALU.mult
                                        ).then_inc(gate_step, 1)
                dve.wait_ge(gate_step, step(3))
                nc.vector.tensor_reduce(gm[:, 3, ts], gates[:, ts], AX_X, ALU.max).then_inc(gate_step, 1)
                dve.wait_ge(gate_step, step(4))
                nc.vector.tensor_tensor(gd[:, ts], gates[:, ts], spread(gm[:, 3], part), ALU.subtract
                                        ).then_inc(gate_step, 1)

            def top2(part):
                ts, w = part.ts, part.width
                step = lambda k: part.whole(GATE_STEPS, 6 + k)
                mine = gates[:, ts].unsqueeze(3).to_broadcast([P, w, NEXP, NEXP])
                other = gates[:, ts].unsqueeze(2).to_broadcast([P, w, NEXP, NEXP])
                lower = cst[:, C_LOWER:C_LOWER + NEXP * NEXP].rearrange("p (e j) -> p e j", e=NEXP)
                nc.vector.tensor_tensor(ties[:, ts], other, mine, ALU.is_equal).then_inc(gate_step, 1)
                nc.vector.tensor_tensor(beats[:, ts], other, mine, ALU.is_gt).then_inc(gate_step, 1)
                dve.wait_ge(gate_step, step(2))
                nc.vector.tensor_tensor(ties[:, ts], ties[:, ts],
                                        lower.unsqueeze(1).to_broadcast([P, w, NEXP, NEXP]),
                                        ALU.mult).then_inc(gate_step, 1)
                dve.wait_ge(gate_step, step(3))
                nc.vector.tensor_tensor(beats[:, ts], beats[:, ts], ties[:, ts], ALU.add).then_inc(gate_step, 1)
                dve.wait_ge(gate_step, step(4))
                nc.vector.tensor_reduce(rank[:, ts], beats[:, ts], AX_X, ALU.add).then_inc(gate_step, 1)
                dve.wait_ge(gate_step, step(5))
                dve.wait_ge(gate_exp, part.whole(2, 1))
                nc.vector.scalar_tensor_tensor(out=gw[:, ts], in0=rank[:, ts], scalar=float(TOPK) - 0.5,
                                               in1=ge[:, ts], op0=ALU.is_lt, op1=ALU.mult).then_inc(gate_step, 1)
                dve.wait_ge(gate_step, step(6))
                nc.vector.tensor_reduce(gm[:, 1, ts], gw[:, ts], AX_X, ALU.add).then_inc(gate_step, 1)
                dve.wait_ge(gate_step, step(7))
                nc.vector.reciprocal(gm[:, 2, ts], gm[:, 1, ts]).then_inc(gate_step, 1)
                dve.wait_ge(gate_step, step(8))
                nc.vector.tensor_tensor(gw[:, ts], gw[:, ts], spread(gm[:, 2], part), ALU.mult
                                        ).then_inc(gate_step, 1)
                dve.wait_ge(gate_step, step(9))
                nc.vector.tensor_copy(gw_hi[:, ts], gw[:, ts]).then_inc(gate_step, 1)
                dve.wait_ge(gate_step, step(10))
                for k in range(2):
                    nc.vector.tensor_copy(w_ext[:, ts, k * NEXP:(k + 1) * NEXP], gw_hi[:, ts].bitcast(F32))
                nc.vector.tensor_tensor(w_ext[:, ts, 2 * NEXP:3 * NEXP], gw[:, ts], gw_hi[:, ts].bitcast(F32),
                                        ALU.subtract).then_inc(gate_ready, 1)

            def result(part):
                dve.wait_ge(out_mm, part.count(1, 0))
                dve.wait_ge(y_free, part.n + 1)
                nc.vector.scalar_tensor_tensor(out=y[:, part.cols], in0=ps(part, OUT_BANK),
                                               scalar=bcol[:, B_OUT:B_OUT + 1], in1=x1[:, part.cols],
                                               op0=ALU.add, op1=ALU.add).then_inc(out_ready, 1)

            def stage(part, name, k):
                if name == "conv":
                    conv(part, k)
                if name == "merge":
                    merge(part)
                if name == "tokens":
                    tokens(part)
                if name == "normalise":
                    normalise_x1(part)
                if name == "features":
                    features(part)
                if name == "logits":
                    logits(part)
                if name == "gate":
                    gate(part)
                if name == "softmax":
                    softmax(part)
                if name == "top2":
                    top2(part)
                if name == "mlp":
                    mlp(part, k)
                if name == "out":
                    result(part)

            nc.vector.memset(warm[:], 0.0).then_inc(warm_ready, 1)
            moments_x(0)
            for c in range(CHUNKS):
                g = c // 2
                if c % 2 == 0:
                    split_x2(g)
                    split_chunk(0, c)
                    normalise(g + 1, g % 2, work[:, nth["x"][g] % PIECE_RING, :], ztmp[:, g % 2, :], range(T))
                else:
                    split_chunk(0, c)
                    split_z(g)
                    if g + 1 < XG:
                        moments_x(g + 1)
            dve.wait_ge(const_landed, 80)
            nc.vector.tensor_scalar(scale[:], bbc[:, NEXP:NEXP + 2], 1.0, 1.0, ALU.add, ALU.add
                                    ).then_inc(setup_done, 1)
            nc.vector.tensor_copy(brow_hi[:], brow[:]).then_inc(setup_step, 1)
            dve.wait_ge(setup_step, 1)
            nc.vector.tensor_tensor(brow_lo[:], brow[:], brow_hi[:].bitcast(F32), ALU.subtract
                                    ).then_inc(setup_step, 1)
            dve.wait_ge(setup_step, 2)
            nc.vector.tensor_scalar(brow_lo[:], brow_lo[:], cst[0:WROWS, C_PART + 1:C_PART + 2], None, ALU.mult
                                    ).then_inc(setup_step, 1)
            dve.wait_ge(setup_step, 3)
            nc.vector.scalar_tensor_tensor(out=brow_ext[:], in0=brow_hi[:].bitcast(F32),
                                           scalar=cst[0:WROWS, C_PART:C_PART + 1], in1=brow_lo[:],
                                           op0=ALU.mult, op1=ALU.add).then_inc(setup_done, 1)
            dve.wait_ge(setup_done, 5)
            with dve.Fori(1, NB) as b:
                for c in range(CHUNKS + LEAD):
                    if c < CHUNKS:
                        split_chunk(b, c)
                    if c == LEAD - 1:
                        aggregated(b - 1)
                    for name, k, at in STAGES:
                        if at == c - LEAD:
                            stage(Part(b - 1), name, k)
            aggregated(NB - 1)
            for name, k, _ in STAGES:
                for part in parts_of(NB - 1, name):
                    stage(part, name, k)

        @block.tensor
        def _(pe):
            def hi_passes(dst, k, xh, start):
                nc.tensor.matmul(dst, wtile(w_hi, k), xh, start=start, stop=False)
                nc.tensor.matmul(dst, wtile(w_lo, k), xh, start=False, stop=False)

            def lo_pass(dst, k, xl, stop):
                return nc.tensor.matmul(dst, wtile(w_hi, k), xl, start=False, stop=stop)

            def aggregate(b, c, v):
                pe.wait_ge(adj_lo_ready, b * CHUNKS + (c + 1))
                if c == 0 and not peeled(b):
                    pe.wait_ge(agg_lo, b * 2 + (v - 1))
                for k in range(CW):
                    zh = z_hi[:, CW * c + k, v * P:(v + 1) * P]
                    zl = z_lo[:, CW * c + k, v * P:(v + 1) * P]
                    ah = adj_hi[:, c % SPLIT_RING, k * ROWS:(k + 1) * ROWS]
                    al = adj_lo[:, c % SPLIT_RING, k * ROWS:(k + 1) * ROWS]
                    nc.tensor.matmul(agg[v], zh, ah, start=(c == 0 and k == 0), stop=False)
                    nc.tensor.matmul(agg[v], zl, ah, start=False, stop=False)
                    ins = nc.tensor.matmul(agg[v], zh, al, start=False, stop=(c == CHUNKS - 1 and k == CW - 1))
                return ins

            def conv(part, s):
                for v in range(2):
                    k, dst = LAYERS * v + s, ps(part, CONV_BANK[s][v])
                    if s == 0:
                        pe.wait_ge(agg_lo, part.n * 2 + (v + 1))
                    else:
                        pe.wait_ge(conv_hi, part.count(6, 2 * s - 2, v, 2))
                    hi_passes(dst, k, act_hi[:, v, part.cols], True)
                    if s > 0:
                        pe.wait_ge(conv_lo, part.count(6, 2 * s - 2, v, 2))
                    lo_pass(dst, k, act_lo[:, v, part.cols], True).then_inc(conv_mm, 1)

            def merge(part):
                dst = ps(part, MERGE_BANK)
                for v in range(2):
                    pe.wait_ge(conv_hi, part.count(6, 4, v, 2))
                    hi_passes(dst, W_MERGE + v, act_hi[:, v, part.cols], v == 0)
                    pe.wait_ge(conv_lo, part.count(6, 4, v, 2))
                    ins = lo_pass(dst, W_MERGE + v, act_lo[:, v, part.cols], v == 1)
                ins.then_inc(merge_mm, 1)

            def tokens(part):
                pe.wait_ge(x1_ready, part.count(1, 0))
                bank = banks[:, part.banks["ABCD".index(TOKENS_BANK)], :]
                for t in part.tiles:
                    ins = nc.tensor.transpose(bank[:, tile_cols(t)], x1[:, tile_cols(t)], cst[:, C_ID:C_ID + P])
                ins.then_inc(tokens_mm, 1)

            def features(part):
                pe.wait_ge(ln_done, part.count(1, 0) + XG)
                bank = banks[:, part.banks["ABCD".index(FEATURES_BANK)], :]
                for t in part.tiles:
                    ins = nc.tensor.transpose(bank[:, tile_cols(t)], ln_x1[:, tile_cols(t)], cst[:, C_ID:C_ID + P])
                ins.then_inc(lnT_mm, 1)

            def logits(part):
                pe.wait_ge(lnT_hi, part.count(1, 0))
                pe.wait_ge(lnT_lo, part.count(1, 0))
                for i, t in enumerate(part.tiles):
                    dst = gate_ps(part)[:, i].rearrange("p k e -> p (k e)")
                    nc.tensor.matmul(dst, act_hi[:, 3, tile_cols(t)], w_gate[:], start=True, stop=False,
                                     skip_group_check=True)
                    ins = nc.tensor.matmul(dst[:, 0:NEXP], act_lo[:, 3, tile_cols(t)], w_gate[:, 0:NEXP],
                                           start=False, stop=True, skip_group_check=True)
                ins.then_inc(logits_mm, 1)

            def mlp(part, j):
                dst = ps(part, MLP_BANK[j])
                if j == 3:
                    pe.wait_ge(logits_step, part.count(2, 0, 1, 2))
                if j == 4:
                    pe.wait_ge(mlp_h, part.count(8, 0))
                if j <= NEXP:
                    k = W_SHARED if j == 0 else W_EXP1 + j - 1
                    hi_passes(dst, k, act_hi[:, 3, part.cols], True)
                    lo_pass(dst, k, act_lo[:, 3, part.cols], True).then_inc(mlp_mm, 1)
                elif j == 5:
                    pe.wait_ge(mlp_h, part.count(8, 1))
                    pe.wait_ge(shared_lo, part.count(2, 0))
                    hi_passes(dst, W_SHARED + 1, act_hi[:, 0, part.cols], True)
                    lo_pass(dst, W_SHARED + 1, act_lo[:, 0, part.cols], True).then_inc(mlp_mm, 1)
                else:
                    q = j - 6
                    pe.wait_ge(mlp_h, part.count(8, 2 * q + 2))
                    for i in range(2):
                        e = 2 * q + i
                        ins = nc.tensor.matmul(dst[i * EH:(i + 1) * EH], w_exp2[:, e * EH:(e + 1) * EH],
                                               work[:, e, part.cols], start=True, stop=True)
                    ins.then_inc(mlp_mm, 1)

            def rows(part):
                pe.wait_ge(mlp_h, part.both(8, 3))
                pe.wait_ge(gate_ready, part.whole(1, 0))
                bank = banks[:, part.banks["ABCD".index(ROWS_BANK)], :]
                for t in part.tiles:
                    ins = nc.tensor.transpose(bank[0:WROWS, tile_cols(t)], w_ext[:, t, :], cst[:, C_ID:C_ID + P])
                ins.then_inc(wT_mm, 1)

            def spread_weights(part):
                pe.wait_ge(wT_ready, part.whole(1, 0))
                for q in range(2):
                    if q == 1:
                        pe.wait_ge(mlp_h, part.both(8, 5))
                    nc.tensor.matmul(spread_ps(part, q), sel[:, tile_cols(q)], wT[:, part.cols],
                                     start=True, stop=True).then_inc(spread_mm, 1)

            def output(part):
                dst = ps(part, OUT_BANK)
                pe.wait_ge(shared_lo, part.count(2, 1))
                pe.wait_ge(mlp_h, part.count(8, 6))
                nc.tensor.matmul(dst, brow_ext[:], wT[:, part.cols], start=True, stop=False)
                hi_passes(dst, W_SHARED + 2, act_hi[:, 0, part.cols], False)
                lo_pass(dst, W_SHARED + 2, act_lo[:, 0, part.cols], False)
                for q in range(2):
                    pe.wait_ge(pair_hi, part.count(2, q))
                    hi_passes(dst, W_EXP3 + q, act_hi[:, 1 + q, part.cols], False)
                    pe.wait_ge(pair_lo, part.count(2, q))
                    ins = lo_pass(dst, W_EXP3 + q, act_lo[:, 1 + q, part.cols], q == 1)
                ins.then_inc(out_mm, 1)

            def stage(part, name, k):
                if name == "conv":
                    conv(part, k)
                if name == "merge":
                    merge(part)
                if name == "tokens":
                    tokens(part)
                if name == "features":
                    features(part)
                if name == "logits":
                    logits(part)
                if name == "mlp":
                    mlp(part, k)
                if name == "rows":
                    rows(part)
                if name == "spread":
                    spread_weights(part)
                if name == "out":
                    output(part)

            for g in range(XG):
                for v in ((1, 0) if g < XG - 1 else (0, 1)):
                    if v == 1:
                        pe.wait_ge(x2_lo, g + 1)
                    else:
                        pe.wait_ge(z_lo_ready, g + 1)
                    for c in (2 * g, 2 * g + 1):
                        ins = aggregate(0, c, v)
                        if v == (0 if g < XG - 1 else 1):
                            ins.then_inc(adj_used, 1)
                        elif c == CHUNKS - 1:
                            ins.then_inc(agg_half_done, 1)
            pe.wait_ge(w_lo_ready, WPIECES)
            pe.wait_ge(setup_done, 5)
            with pe.Fori(1, NB) as b:
                for c, v, step in PASSES:
                    ins = aggregate(b, c, v)
                    if v == 1:
                        ins.then_inc(adj_used, 1)
                    elif c == CHUNKS - 1:
                        ins.then_inc(agg_half_done, 1)
                    for name, k, at in STAGES:
                        if at == step:
                            stage(Part(b - 1), name, k)
            for name, k, _ in STAGES:
                for part in parts_of(NB - 1, name):
                    stage(part, name, k)


def _layout(a):
    import numpy as np

    n = a["adj"].shape[0]
    nb = n // ROWS
    adj = a["adj"].reshape(nb, P, T, nb, P, T).transpose(0, 4, 3, 5, 2, 1).reshape(nb * P, n * T)

    eW3 = a["L0_ffn_eW3"]
    weights = np.concatenate(
        [a["L0_gnn_W1"][k].T for k in range(LAYERS)] + [a["L0_gnn_W2"][k].T for k in range(LAYERS)]
        + [a["L0_gnn_Wm"][:, :P].T, a["L0_gnn_Wm"][:, P:].T]
        + [a["L0_ffn_sW1"], a["L0_ffn_sW2"], a["L0_ffn_sW3"]]
        + [a["L0_ffn_eW1"][e] for e in range(NEXP)]
        + [eW3[2 * q:2 * q + 2].reshape(P, P) for q in range(NEXP // 2)] + [a["L0_ffn_gW"]], axis=1)
    bias_cols = np.concatenate([a["L0_gnn_b1"], a["L0_gnn_b2"], a["L0_ffn_sb1"][None], a["L0_ffn_sb2"][None],
                                a["L0_ffn_eb1"], a["L0_ffn_eb2"].reshape(NEXP // 2, P),
                                a["L0_gnn_bm"][None], a["L0_ffn_sb3"][None]]).T
    bias_bc = np.concatenate([a["L0_ffn_gb"], a["L0_gnn_eps1"], a["L0_gnn_eps2"]])
    bias_rows = np.concatenate([a["L0_ffn_eb3"]] * 3)

    consts = np.zeros((P, C_COLS), np.float32)
    consts[:, C_ID:C_ID + P] = np.eye(P)
    for e in range(NEXP):
        for row in (e, 2 * NEXP + e):
            consts[row, C_SEL + 64 * e:C_SEL + 64 * (e + 1)] = 1
    consts[:, C_LOWER:C_PART] = np.tril(np.ones((NEXP, NEXP)), -1).reshape(-1)
    hi_rows = np.array([1] * NEXP + [0] * NEXP + [1] * NEXP)
    consts[:WROWS, C_PART] = hi_rows
    consts[:WROWS, C_PART + 1] = 1 - hi_rows
    xT = a["x"].reshape(nb, P, T, P).transpose(3, 0, 2, 1).reshape(P, n)
    return {"adj": adj, "x": a["x"], "xT": xT, "x2": a["L0_gnn_x2"], "weights": weights,
            "w_exp2": a["L0_ffn_eW2"].transpose(1, 0, 2).reshape(P, NEXP * EH), "bias_cols": bias_cols,
            "bias_bc": bias_bc, "bias_rows": bias_rows, "consts": consts}


def kernel(**inputs):
    import numpy as _np
    import concourse.bacc as _bacc
    from concourse import mybir as _mybir
    from concourse.bass_utils import run_bass_kernel_spmd as _run

    nc = _bacc.Bacc("TRN2", target_bir_lowering=False, num_devices=1)
    arrays, args = {}, []
    for name, a in _layout({k: _np.asarray(v) for k, v in inputs.items()}).items():
        a = _np.ascontiguousarray(a)
        arrays[f"in_{name}_dram"] = a
        args.append(nc.dram_tensor(f"in_{name}_dram", a.shape, _mybir.dt.from_np(a.dtype), kind="ExternalInput").ap())
    rows, width = inputs["x"].shape
    args.append(nc.dram_tensor("out_0_dram", (width, rows), _mybir.dt.float32, kind="ExternalOutput").ap())
    gnn_moe_kernel(nc, *args)
    r = _run(nc, [arrays], core_ids=[0])
    got = r.results[0]["out_0_dram"].reshape(width, rows // ROWS, T, P)
    return _np.ascontiguousarray(got.transpose(1, 3, 2, 0).reshape(rows, width))
```

```python
from contextlib import ExitStack

import concourse.bass as bass
from concourse import mybir

F32 = mybir.dt.float32
F32R = mybir.dt.float32r
ALU = mybir.AluOpType
ACT = mybir.ActivationFunctionType
AX_X = mybir.AxisListType.X

P = 128
T = 4
ROWS = T * P
NEXP = 4
EH = 64
TOPK = 2
LAYERS = 3
CW = 2
RAW_RING = 8
SPLIT_RING = 4
PIECE_RING = 7
PIECE_LEAD = 6
LN_EPS = 1e-5
WROWS = 3 * NEXP

W_MERGE = 2 * LAYERS
W_SHARED = W_MERGE + 2
W_EXP1 = W_SHARED + 3
W_EXP3 = W_EXP1 + NEXP
W_GATE = W_EXP3 + NEXP // 2
W_COLS = W_GATE * P + NEXP

B_SH = 2 * LAYERS
B_EXP1 = B_SH + 2
B_EXP2 = B_EXP1 + NEXP
B_MERGE = B_EXP2 + NEXP // 2
B_OUT = B_MERGE + 1
B_COLS = B_OUT + 1

C_ID = 0
C_SEL = P
C_LOWER = C_SEL + 2 * P
C_PART = C_LOWER + NEXP * NEXP
C_COLS = C_PART + 2

STAGES = (
    ("conv", 0, 0), ("conv", 1, 2), ("conv", 2, 4), ("merge", 0, 6), ("tokens", 0, 7),
    ("normalise", 0, 7), ("features", 0, 9), ("logits", 0, 10), ("gate", 0, 10),
    ("mlp", 0, 10), ("exp", 0, 10), ("mlp", 1, 10),
    ("softmax", 0, 10), ("exp", 1, 10), ("top2", 0, 10), ("mlp", 2, 11), ("mlp", 3, 11),
    ("mlp", 4, 11), ("rows", 0, 12), ("mlp", 5, 12), ("mlp", 6, 12), ("mlp", 7, 12),
    ("spread", 0, 12), ("out", 0, 14),
)
BOTH = None
LAST = (
    (0, "input", 0), (1, "input", 0), (0, "conv", 0), (1, "conv", 0), (0, "conv", 1),
    (1, "conv", 1), (0, "conv", 2), (1, "conv", 2), (0, "merge", 0), (1, "merge", 0),
    (0, "tokens", 0), (1, "tokens", 0), (BOTH, "warm", 8), (0, "normalise", 0), (1, "normalise", 0),
    (0, "features", 0), (1, "features", 0), (0, "logits", 0), (0, "mlp", 0), (1, "logits", 0),
    (BOTH, "gate", 0), (1, "mlp", 0), (BOTH, "exp", 0), (0, "mlp", 1), (0, "mlp", 2),
    (BOTH, "softmax", 0), (0, "mlp", 3), (BOTH, "exp", 1), (BOTH, "top2", 0), (1, "mlp", 1),
    (1, "mlp", 2), (1, "mlp", 3), (0, "mlp", 4), (1, "mlp", 4), (1, "mlp", 5), (1, "mlp", 6),
    (0, "mlp", 5), (BOTH, "rows", 0), (0, "mlp", 6), (0, "mlp", 7), (BOTH, "spread", 0),
    (1, "pair", 0), (0, "pair", 0), (1, "mlp", 7), (0, "pair", 1), (1, "pair", 1), (0, "out", 0),
    (1, "out", 0),
)
LEAD = 2
GATE_STEPS = 17


class Part:

    def __init__(self, n, half=None):
        self.n, self.half = n, half
        self.tiles = range(T) if half is None else range(half * T // 2, (half + 1) * T // 2)
        self.cols = slice(self.tiles[0] * P, (self.tiles[-1] + 1) * P)
        self.ts = slice(self.tiles[0], self.tiles[-1] + 1)
        self.width = len(self.tiles)
        self.norm = n + (2 if half == 1 else 1)

    def count(self, per, before, k=0):
        return self.n * per + (before + k + 1)


def gnn_moe_kernel(nc, adj, x, xT, x2, weights, w_exp2_in, bias_cols, bias_bc, bias_rows, consts, out):
    NB, NODES = adj.shape[0] // P, adj.shape[1] // ROWS
    CHUNKS = NODES // CW
    CCOLS = CW * ROWS
    XG = NODES // T
    WPIECES = -(-W_COLS // ROWS)
    pieces = sorted([(2 * g, k, g) for g in range(XG) for k in ("a x2", "b x")]
                    + [(CHUNKS - 1 - 2 * k, "c w", WPIECES - 1 - k) for k in range(WPIECES)])
    pieces = [(c, kind[2:], k) for c, kind, k in pieces]
    PASSES = [(0, 0, None), (1, 0, 0), (0, 1, None), (1, 1, 1)]
    for c in range(2, CHUNKS - 2):
        PASSES += [(c, 0, None), (c, 1, c)]
    PASSES += [(CHUNKS - 2, 0, CHUNKS - 2), (CHUNKS - 1, 0, None),
               (CHUNKS - 2, 1, None), (CHUNKS - 1, 1, CHUNKS - 1)]
    nth = {kind: [i for i, p in enumerate(pieces) if p[1] == kind] for kind in ("x", "x2", "w")}

    with ExitStack() as ctx:
        def sb(name, shape, dt=F32):
            return ctx.enter_context(nc.sbuf_tensor(name, shape, dt))

        def sem(name):
            return ctx.enter_context(nc.semaphore(name))

        z_hi = sb("z_hi", [P, NODES, 2 * P], F32R)
        z_lo = sb("z_lo", [P, NODES, 2 * P], F32R)
        adj_raw = sb("adj_raw", [P, RAW_RING, CCOLS])
        adj_hi = sb("adj_hi", [P, SPLIT_RING, CCOLS], F32R)
        adj_lo = sb("adj_lo", [P, SPLIT_RING, CCOLS], F32R)
        w_hi = sb("w_hi", [P, W_COLS], F32R)
        w_lo = sb("w_lo", [P, W_COLS], F32R)
        w_gate = sb("w_gate", [P, 2 * NEXP], F32R)
        w_exp2 = sb("w_exp2", [P, NEXP * EH])
        act_hi = sb("act_hi", [P, 4, ROWS], F32R)
        act_lo = sb("act_lo", [P, 4, ROWS], F32R)
        work = sb("work", [P, 9, ROWS])
        whole = [work[:, 4 + k, :] for k in range(3)]
        ztmp = work[:, 7:9, :]
        x1, ln_x1 = work[:, 7, :], work[:, 8, :]
        xres = sb("xres", [P, ROWS])
        y = sb("y", [P, ROWS])
        wT = sb("wT", [WROWS, ROWS], F32R)
        cst = sb("cst", [P, C_COLS])
        sel = sb("sel", [WROWS, 2 * P], F32R)
        bcol = sb("bcol", [P, B_COLS])
        bbc = sb("bbc", [P, NEXP + 2])
        brow = sb("brow", [WROWS, P])
        brow_hi = sb("brow_hi", [WROWS, P], F32R)
        brow_lo = sb("brow_lo", [WROWS, P])
        brow_ext = sb("brow_ext", [WROWS, P], F32R)
        scale = sb("scale", [P, 2])
        stats = sb("stats", [P, 2, T, 6])
        mv = sb("mv", [P, 2, T, 2])
        var = sb("var", [P, 2, T])
        rstd = sb("rstd", [P, 2, T])
        mhalf = sb("mhalf", [P, T])
        eps = sb("eps", [P, T])
        waiter = sb("waiter", [P, 2])
        warm = sb("warm", [P, 2])
        freed = sb("freed", [P, 1])
        gl = sb("gl", [P, T, NEXP])
        gm = sb("gm", [P, 4, T])
        gd = sb("gd", [P, T, NEXP])
        ge = sb("ge", [P, T, NEXP])
        gates = sb("gates", [P, T, NEXP])
        beats = sb("beats", [P, T, NEXP, NEXP])
        ties = sb("ties", [P, T, NEXP, NEXP])
        rank = sb("rank", [P, T, NEXP])
        gw = sb("gw", [P, T, NEXP])
        gw_hi = sb("gw_hi", [P, T, NEXP], F32R)
        w_ext = sb("w_ext", [P, T, WROWS])

        banks = ctx.enter_context(nc.psum_tensor("banks", [P, 8, ROWS], F32))
        agg = [banks[:, v, :] for v in range(2)]

        def ps(part, which):
            return banks[:, 2 + "ABCD".index(which), part.cols]

        CONV_BANK = (("A", "B"), ("C", "D"), ("A", "B"))
        MERGE_BANK, TOKENS_BANK, FEATURES_BANK, GATE_BANK = "C", "D", "A", "B"
        MLP_BANK = "CDABCDAC"
        ROWS_BANK, SPREAD_BANK, OUT_BANK = "B", ("B", "D"), "A"

        def spread_ps(part, q):
            return ps(part, SPREAD_BANK[q])

        def gate_ps(part):
            b = ps(part, GATE_BANK)[:, 0:T * 2 * NEXP]
            return b.rearrange("p (t k e) -> p t k e", t=T, k=2)

        adj_landed = [sem(f"adj_landed{k}") for k in range(RAW_RING)]
        piece_landed = [sem(f"piece_landed{k}") for k in range(PIECE_RING)]
        const_landed, xres_landed = sem("const_landed"), sem("xres_landed")
        y_free, stored, last_stored = sem("y_free"), sem("stored"), sem("last_stored")
        adj_hi_ready, adj_lo_ready, adj_used = sem("adj_hi_ready"), sem("adj_lo_ready"), sem("adj_used")
        z_hi_ready, z_lo_ready = sem("z_hi_ready"), sem("z_lo_ready")
        x2_hi, x2_lo, w_hi_ready, w_lo_ready = sem("x2_hi"), sem("x2_lo"), sem("w_hi_ready"), sem("w_lo_ready")
        ln_part, ln_stats, rstd_step, rstd_ready, ln_done = (
            sem("ln_part"), sem("ln_stats"), sem("rstd_step"), sem("rstd_ready"), sem("ln_done"))
        setup_step, dve_setup, act_setup, eps_ready, warm_ready = (
            sem("setup_step"), sem("dve_setup"), sem("act_setup"), sem("eps_ready"), sem("warm_ready"))
        agg_half_done, agg_hi, agg_lo = sem("agg_half_done"), sem("agg_hi"), sem("agg_lo")
        conv_mm, conv_hi, conv_lo = sem("conv_mm"), sem("conv_hi"), sem("conv_lo")
        conv_whole = [sem("conv_whole_act"), sem("conv_whole_dve")]
        merge_mm, x1_ready, tokens_mm = sem("merge_mm"), sem("x1_ready"), sem("tokens_mm")
        lnT_mm, lnT_hi, lnT_lo = sem("lnT_mm"), sem("lnT_hi"), sem("lnT_lo")
        logits_mm, logits_step, gate_step, gate_exp, gate_ready = (
            sem("logits_mm"), sem("logits_step"), sem("gate_step"), sem("gate_exp"), sem("gate_ready"))
        wT_mm, wT_ready, spread_mm = sem("wT_mm"), sem("wT_ready"), sem("spread_mm")
        mlp_mm, mlp_h = sem("mlp_mm"), sem("mlp_h")
        shared_hi, shared_lo = sem("shared_hi"), sem("shared_lo")
        pair_gated, pair_hi, pair_lo = sem("pair_gated"), sem("pair_hi"), sem("pair_lo")
        out_mm, out_ready = sem("out_mm"), sem("out_ready")

        def of_halves(name):
            return [sem(f"{name}_half{h}") for h in range(2)]

        last_weights = sem("last_weights")
        last_conv_in = [of_halves(f"last_conv{v}_in") for v in range(2)]
        last_conv_mm = [of_halves(f"last_conv{v}_mm") for v in range(2)]
        last_merge_mm, last_x1, last_tokens_mm = (
            of_halves("last_merge_mm"), of_halves("last_x1"), of_halves("last_tokens_mm"))
        last_lnT_mm, last_lnT_hi, last_lnT_lo = (
            of_halves("last_lnT_mm"), of_halves("last_lnT_hi"), of_halves("last_lnT_lo"))
        last_logits_mm, last_logits = of_halves("last_logits_mm"), of_halves("last_logits")
        last_mlp_mm, last_mlp_h, last_gated = (
            of_halves("last_mlp_mm"), of_halves("last_mlp_h"), of_halves("last_gated"))
        last_rows_mm, last_rows, last_spread_mm = sem("last_rows_mm"), sem("last_rows"), sem("last_spread_mm")
        last_out_mm, last_out = of_halves("last_out_mm"), of_halves("last_out")

        x_rows = x.rearrange("(b p t) f -> b p (t f)", p=P, t=T)
        x2_rows = x2.rearrange("(b p t) f -> b p (t f)", p=P, t=T)

        def wtile(w, k):
            return w[:, k * P:(k + 1) * P]

        def tile_cols(t):
            return slice(t * P, (t + 1) * P)

        def weight_cols(k):
            return k * ROWS, min(W_COLS, (k + 1) * ROWS)

        def piece_source(i):
            _, kind, k = pieces[i]
            if kind == "w":
                return weights[:, slice(*weight_cols(k))]
            return (x_rows if kind == "x" else x2_rows)[k]

        def node_group(g):
            return slice(T * g, T * g + T)

        def by_tile(ap):
            return ap.rearrange("p (t f) -> p t f", f=P)

        def spread(ap, part):
            return ap[:, part.ts].unsqueeze(2).to_broadcast([P, part.width, NEXP])

        def peeled(b):
            return isinstance(b, int)

        W_SLOTS = -(-W_COLS // CCOLS)
        w_plain = adj_raw[:, 0:W_SLOTS, :].rearrange("p k c -> p (k c)")
        halves = [Part(NB - 1, h) for h in range(2)]
        last_block = Part(NB - 1)

        LAST_BANKS = ((0, 3, 5, 2), (1, 4, 7, 6))

        def last_ps(which, part):
            return banks[:, LAST_BANKS[part.half]["WXYZ".index(which)], part.cols]

        LAST_CONV, LAST_MERGE, LAST_TOKENS, LAST_FEATURES, LAST_GATE = "XY", "Z", "X", "Y", "W"
        LAST_MLP = "ZXYWZXYW"
        last_rows_bank, last_spread_bank, last_out_bank = 2, (6, 3), (2, 4)

        def last_gate_ps(part):
            b = last_ps(LAST_GATE, part)[:, 0:part.width * 2 * NEXP]
            return b.rearrange("p (t k e) -> p t k e", t=part.width, k=2)

        def last_stages(functions):
            for half, name, k in LAST:
                if name in functions:
                    part = last_block if half is BOTH else halves[half]
                    functions[name](part, k)

        block = ctx.enter_context(nc.Block())

        @block.sync
        def _(sp):
            def load_chunk(b, c):
                if not (peeled(b) and c < RAW_RING):
                    sp.wait_ge(adj_hi_ready, b * CHUNKS + (c + 1 - RAW_RING))
                    sp.wait_ge(adj_lo_ready, b * CHUNKS + (c + 1 - RAW_RING))
                sp.dma_start(adj_raw[:, c % RAW_RING, :],
                             adj[bass.ds(b * P, P), c * CCOLS:(c + 1) * CCOLS]
                             ).then_inc(adj_landed[c % RAW_RING], 16)

            def load_piece(i):
                _, old, k = pieces[i - PIECE_RING]
                sp.wait_ge({"x": ln_done, "x2": x2_lo, "w": w_lo_ready}[old], k + 1)
                if old != "x":
                    sp.wait_ge({"x2": x2_hi, "w": w_hi_ready}[old], k + 1)
                src = piece_source(i)
                sp.dma_start(work[:, i % PIECE_RING, 0:src.shape[1]], src).then_inc(piece_landed[i % PIECE_RING], 16)

            def load_xres(n):
                sp.wait_ge(agg_lo, n * 2 + 1)
                sp.dma_start(xres[:], xT[:, bass.ds(n * ROWS, ROWS)]).then_inc(xres_landed, 16)

            for i in range(PIECE_RING):
                sp.dma_start(work[:, i, :], piece_source(i)).then_inc(piece_landed[i], 16)
                if i % 2 == 0:
                    load_chunk(0, i // 2)
            first_chunks = (PIECE_RING + 1) // 2
            sp.dma_start(cst[:], consts).then_inc(const_landed, 16)
            sp.dma_start(bcol[:], bias_cols).then_inc(const_landed, 16)
            sp.dma_start(bbc[:], bias_bc.partition_broadcast(P)).then_inc(const_landed, 16)
            sp.dma_start(brow[:], bias_rows).then_inc(const_landed, 16)
            sp.dma_start(w_exp2[:], w_exp2_in).then_inc(const_landed, 16)
            loaded = PIECE_RING
            for c in range(first_chunks, CHUNKS):
                load_chunk(0, c)
                while loaded < len(pieces) and pieces[loaded - PIECE_RING][0] <= c - PIECE_LEAD:
                    load_piece(loaded)
                    loaded += 1
            for i in range(loaded, len(pieces)):
                load_piece(i)
            with sp.Fori(1, NB) as b:
                for c in range(CHUNKS):
                    load_chunk(b, c)
                    if c == RAW_RING + 1:
                        load_xres(b - 1)
            last = (NB - 1) * CHUNKS + CHUNKS - RAW_RING + W_SLOTS
            sp.wait_ge(adj_hi_ready, last)
            sp.wait_ge(adj_lo_ready, last)
            sp.dma_start(w_plain[:, 0:W_COLS], weights).then_inc(last_weights, 16)
            sp.wait_ge(adj_lo_ready, NB * CHUNKS)
            sp.dma_start(xres[:], xT[:, (NB - 1) * ROWS:NB * ROWS]).then_inc(xres_landed, 16)
            for part in halves:
                sp.wait_ge(last_out[part.half], 1)
                sp.dma_start(out[:, (NB - 1) * ROWS + part.cols.start:(NB - 1) * ROWS + part.cols.stop],
                             y[:, part.cols]).then_inc(last_stored, 16)
            sp.wait_ge(last_stored, 32)

        @block.gpsimd
        def _(pool):
            nc.gpsimd.memset(eps[:], LN_EPS).then_inc(y_free, 1)
            nc.gpsimd.memset(mhalf[:], -0.5).then_inc(eps_ready, 1)
            pool.wait_ge(y_free, 1)
            pool.wait_ge(eps_ready, 1)

            def inverse_std(k, slot, ts):
                pool.wait_ge(ln_stats, k)
                nc.gpsimd.tensor_tensor(var[:, slot, ts], mv[:, slot, ts, 1], eps[:, ts], ALU.add
                                        ).then_inc(rstd_step, 1)
                pool.wait_ge(rstd_step, k)
                nc.gpsimd.tensor_tensor(rstd[:, slot, ts], var[:, slot, ts], mhalf[:, ts], ALU.pow
                                        ).then_inc(rstd_ready, 1)

            def split_x2(g):
                i = nth["x2"][g]
                pool.wait_ge(x2_hi, g + 1)
                nc.gpsimd.tensor_tensor(z_lo[:, node_group(g), P:2 * P], by_tile(work[:, i % PIECE_RING, :]),
                                        z_hi[:, node_group(g), P:2 * P].bitcast(F32), ALU.subtract
                                        ).then_inc(x2_lo, 1)

            for g in range(XG):
                split_x2(g)
                inverse_std(g + 1, g % 2, slice(0, T))
                for i in nth["w"]:
                    if pieces[i][0] in (2 * g, 2 * g + 1):
                        lo, hi = weight_cols(pieces[i][2])
                        pool.wait_ge(w_hi_ready, pieces[i][2] + 1)
                        nc.gpsimd.tensor_tensor(w_lo[:, lo:hi], work[:, i % PIECE_RING, 0:hi - lo],
                                                w_hi[:, lo:hi].bitcast(F32), ALU.subtract
                                                ).then_inc(w_lo_ready, 1)
            with pool.Fori(0, NB - 1) as n:
                inverse_std(n + (XG + 1), 0, slice(0, T))
                pool.wait_ge(out_ready, n + 1)
                pool.dma_start(out[:, bass.ds(n * ROWS, ROWS)], y[:]).then_inc(stored, 16)
                pool.wait_ge(stored, n * 16 + 16)
                nc.gpsimd.tensor_tensor(freed[:], eps[:, 0:1], eps[:, 0:1], ALU.add).then_inc(y_free, 1)
            for part in halves:
                inverse_std(part.norm + XG, 0, part.ts)

        @block.scalar
        def _(act):
            def split_piece(i):
                _, kind, k = pieces[i]
                act.wait_ge(piece_landed[i % PIECE_RING], 16 * (i // PIECE_RING + 1))
                if kind == "x2":
                    nc.scalar.activation(z_hi[:, node_group(k), P:2 * P], by_tile(work[:, i % PIECE_RING, :]),
                                         ACT.Copy).then_inc(x2_hi, 1)
                else:
                    lo, hi = weight_cols(k)
                    nc.scalar.activation(w_hi[:, lo:hi], work[:, i % PIECE_RING, 0:hi - lo], ACT.Copy
                                         ).then_inc(w_hi_ready, 1)

            def split_chunk(b, c):
                act.wait_ge(adj_landed[c % RAW_RING], b * (16 * CHUNKS // RAW_RING) + 16 * (c // RAW_RING + 1))
                if not (peeled(b) and c < SPLIT_RING):
                    act.wait_ge(adj_used, b * CHUNKS + (c + 1 - SPLIT_RING))
                nc.scalar.activation(adj_hi[:, c % SPLIT_RING, :], adj_raw[:, c % RAW_RING, :], ACT.Copy
                                     ).then_inc(adj_hi_ready, 1)

            def split_z(g):
                act.wait_ge(ln_done, g + 1)
                nc.scalar.activation(z_hi[:, node_group(g), 0:P], by_tile(ztmp[:, g % 2, :]), ACT.Copy
                                     ).then_inc(z_hi_ready, 1)

            def aggregated(n):
                for v in range(2):
                    if v == 0:
                        act.wait_ge(agg_half_done, n + 1)
                    else:
                        act.wait_ge(adj_used, n * CHUNKS + CHUNKS)
                    nc.scalar.activation(act_hi[:, v, :], agg[v], ACT.Copy, scale=scale[:, v:v + 1]
                                         ).then_inc(agg_hi, 1)

            def conv(part, s):
                for v in range(2):
                    bias = bcol[:, LAYERS * v + s:LAYERS * v + s + 1]
                    act.wait_ge(conv_mm, part.count(6, 2 * s, v))
                    nc.scalar.activation(act_hi[:, v, part.cols], ps(part, CONV_BANK[s][v]), ACT.Relu,
                                         bias=bias).then_inc(conv_hi, 1)
                    if v == 0:
                        nc.scalar.activation(whole[0][:, part.cols], ps(part, CONV_BANK[s][0]), ACT.Relu,
                                             bias=bias).then_inc(conv_whole[0], 1)

            def features(part):
                act.wait_ge(lnT_mm, part.count(1, 0))
                nc.scalar.activation(act_hi[:, 3, part.cols], ps(part, FEATURES_BANK), ACT.Copy).then_inc(lnT_hi, 1)

            def mlp(part, j):
                b = (B_SH, B_EXP1, B_EXP1 + 1, B_EXP1 + 2, B_EXP1 + 3, B_SH + 1, B_EXP2, B_EXP2 + 1)[j]
                dst = (whole[0], work[:, 0, :], work[:, 1, :], work[:, 2, :], work[:, 3, :], whole[0],
                       whole[1], whole[2])[j]
                act.wait_ge(mlp_mm, part.count(8, j))
                if j in (0, 5):
                    nc.scalar.activation(act_hi[:, 0, part.cols], ps(part, MLP_BANK[j]), ACT.Relu,
                                         bias=bcol[:, b:b + 1]).then_inc(shared_hi, 1)
                nc.scalar.activation(dst[:, part.cols], ps(part, MLP_BANK[j]), ACT.Relu,
                                     bias=bcol[:, b:b + 1]).then_inc(mlp_h, 1)

            def exponential(part, which):
                act.wait_ge(gate_step, part.count(GATE_STEPS, 1 if which == 0 else 6))
                nc.scalar.activation(ge[:, part.ts], gd[:, part.ts], ACT.Exp).then_inc(gate_exp, 1)

            def rows(part):
                act.wait_ge(wT_mm, part.count(1, 0))
                nc.scalar.activation(wT[:, part.cols], ps(part, ROWS_BANK)[0:WROWS], ACT.Copy).then_inc(wT_ready, 1)

            def stage(part, name, k):
                if name == "conv":
                    conv(part, k)
                if name == "features":
                    features(part)
                if name == "mlp":
                    mlp(part, k)
                if name == "exp":
                    exponential(part, k)
                if name == "rows":
                    rows(part)

            act.wait_ge(warm_ready, 1)
            nc.scalar.activation(warm[:, 0:1], warm[:, 1:2], ACT.Exp)
            for c in range(CHUNKS):
                for i in nth["x2"] + nth["w"]:
                    if pieces[i][0] == c:
                        split_piece(i)
                split_chunk(0, c)
                if c % 2 == 1:
                    split_z(c // 2)
            act.wait_ge(const_landed, 80)
            nc.scalar.activation(sel[:], cst[0:WROWS, C_SEL:C_SEL + 2 * P], ACT.Copy).then_inc(act_setup, 1)
            act.wait_ge(w_hi_ready, WPIECES)
            nc.scalar.activation(w_gate[:, 0:NEXP], w_hi[:, W_GATE * P:W_COLS].bitcast(F32), ACT.Copy
                                 ).then_inc(act_setup, 1)
            act.wait_ge(w_lo_ready, WPIECES)
            nc.scalar.activation(w_gate[:, NEXP:2 * NEXP], w_lo[:, W_GATE * P:W_COLS].bitcast(F32), ACT.Copy
                                 ).then_inc(act_setup, 1)
            act.wait_ge(dve_setup, 2)
            with act.Fori(1, NB) as b:
                for c in range(CHUNKS + LEAD):
                    if c < CHUNKS:
                        split_chunk(b, c)
                    if c == LEAD - 1:
                        aggregated(b - 1)
                    for name, k, at in STAGES:
                        if at == c - LEAD:
                            stage(Part(b - 1), name, k)
            def last_relu(dst, src, bias_col):
                return nc.scalar.activation(dst, src, ACT.Relu, bias=bcol[:, bias_col:bias_col + 1])

            def last_conv_input(part, _):
                act.wait_ge(agg_half_done, NB)
                nc.scalar.activation(work[:, 4, part.cols], agg[0][:, part.cols], ACT.Copy, scale=scale[:, 0:1]
                                     ).then_inc(last_conv_in[0][part.half], 1)

            def last_conv(part, s):
                act.wait_ge(last_conv_mm[0][part.half], s + 1)
                last_relu(work[:, 4, part.cols], last_ps(LAST_CONV[0], part), s
                          ).then_inc(last_conv_in[0][part.half], 1)

            def last_features(part, _):
                act.wait_ge(last_lnT_mm[part.half], 1)
                nc.scalar.activation(act_hi[:, 3, part.cols], last_ps(LAST_FEATURES, part), ACT.Copy
                                     ).then_inc(last_lnT_hi[part.half], 1)

            def last_mlp(part, j):
                b = (B_SH, B_EXP1, B_EXP1 + 1, B_EXP1 + 2, B_EXP1 + 3, B_SH + 1, B_EXP2, B_EXP2 + 1)[j]
                slot = (4, 0, 1, 2, 3, 4, 5, 6)[j]
                act.wait_ge(last_mlp_mm[part.half], j + 1)
                last_relu(work[:, slot, part.cols], last_ps(LAST_MLP[j], part), b
                          ).then_inc(last_mlp_h[part.half], 1)

            def last_gate_rows(part, _):
                act.wait_ge(last_rows_mm, 1)
                nc.scalar.activation(wT[:], banks[0:WROWS, last_rows_bank, :], ACT.Copy
                                     ).then_inc(last_rows, 1)

            last_stages({"input": last_conv_input, "conv": last_conv, "features": last_features,
                         "exp": exponential, "mlp": last_mlp, "rows": last_gate_rows})

        @block.vector
        def _(dve):
            def split_chunk(b, c):
                dve.wait_ge(adj_hi_ready, b * CHUNKS + (c + 1))
                nc.vector.tensor_tensor(adj_lo[:, c % SPLIT_RING, :], adj_raw[:, c % RAW_RING, :],
                                        adj_hi[:, c % SPLIT_RING, :].bitcast(F32), ALU.subtract
                                        ).then_inc(adj_lo_ready, 1)

            def moments(k, slot, src, tiles):
                for t in tiles:
                    last = nc.vector.bn_stats(stats[:, slot, t, :], src[:, tile_cols(t)])
                last.then_inc(ln_part, 1)
                dve.wait_ge(ln_part, k)
                nc.vector.tensor_copy(waiter[:, 0:1], stats[:, slot, tiles[-1], 0:1])
                for t in tiles:
                    last = nc.vector.bn_aggr(mv[:, slot, t, :], stats[:, slot, t, :])
                last.then_inc(ln_stats, 1)

            def normalise(k, slot, src, dst, tiles):
                dve.wait_ge(rstd_ready, k)
                for t in tiles:
                    last = nc.vector.tensor_scalar(dst[:, tile_cols(t)], src[:, tile_cols(t)],
                                                   mv[:, slot, t, 0:1], rstd[:, slot, t:t + 1],
                                                   ALU.subtract, ALU.mult)
                last.then_inc(ln_done, 1)

            def moments_x(g):
                i = nth["x"][g]
                dve.wait_ge(piece_landed[i % PIECE_RING], 16 * (i // PIECE_RING + 1))
                moments(g + 1, g % 2, work[:, i % PIECE_RING, :], range(T))

            def split_z(g):
                dve.wait_ge(z_hi_ready, g + 1)
                nc.vector.tensor_tensor(z_lo[:, node_group(g), 0:P], by_tile(ztmp[:, g % 2, :]),
                                        z_hi[:, node_group(g), 0:P].bitcast(F32), ALU.subtract
                                        ).then_inc(z_lo_ready, 1)

            def aggregated(n):
                for v in range(2):
                    dve.wait_ge(agg_hi, n * 2 + (v + 1))
                    nc.vector.scalar_tensor_tensor(out=act_lo[:, v, :], in0=agg[v], scalar=scale[:, v:v + 1],
                                                   in1=act_hi[:, v, :].bitcast(F32), op0=ALU.mult,
                                                   op1=ALU.subtract).then_inc(agg_lo, 1)

            def conv(part, s):
                for v in range(2):
                    if v == 0:
                        dve.wait_ge(conv_whole[0], part.count(3, s))
                    else:
                        dve.wait_ge(conv_hi, part.count(6, 2 * s, 1))
                        nc.vector.tensor_scalar(whole[1][:, part.cols], ps(part, CONV_BANK[s][1]),
                                                bcol[:, LAYERS + s:LAYERS + s + 1], 0.0, ALU.add, ALU.max
                                                ).then_inc(conv_whole[1], 1)
                        dve.wait_ge(conv_whole[1], part.count(3, s))
                    nc.vector.tensor_tensor(act_lo[:, v, part.cols], whole[v][:, part.cols],
                                            act_hi[:, v, part.cols].bitcast(F32), ALU.subtract
                                            ).then_inc(conv_lo, 1)

            def merge(part):
                dve.wait_ge(merge_mm, part.count(1, 0))
                dve.wait_ge(xres_landed, part.n * 16 + 16)
                nc.vector.scalar_tensor_tensor(out=x1[:, part.cols], in0=ps(part, MERGE_BANK),
                                               scalar=bcol[:, B_MERGE:B_MERGE + 1], in1=xres[:, part.cols],
                                               op0=ALU.add, op1=ALU.add).then_inc(x1_ready, 1)

            def tokens(part):
                bank = ps(part, TOKENS_BANK)
                dve.wait_ge(tokens_mm, part.count(1, 0))
                nc.vector.tensor_copy(waiter[:, 1:2], bank[:, 0:1])
                moments(part.norm + XG, 0, bank, part.tiles)

            def normalise_x1(part):
                bank = ps(part, TOKENS_BANK)
                normalise(part.norm + XG, 0, bank, ln_x1, part.tiles)

            def features(part):
                dve.wait_ge(lnT_hi, part.count(1, 0))
                nc.vector.tensor_tensor(act_lo[:, 3, part.cols], ps(part, FEATURES_BANK),
                                        act_hi[:, 3, part.cols].bitcast(F32), ALU.subtract).then_inc(lnT_lo, 1)

            def mlp(part, j):
                if 1 <= j <= NEXP:
                    return
                dve.wait_ge(mlp_h, part.count(8, j))
                if j in (0, 5):
                    src, slot, signal = whole[0][:, part.cols], 0, shared_lo
                else:
                    q = j - 6
                    src, slot, signal = whole[1 + q][:, part.cols], 1 + q, pair_lo
                    dve.wait_ge(spread_mm, part.count(2, q))
                    nc.vector.tensor_tensor(src, src, spread_ps(part, q), ALU.mult).then_inc(pair_gated, 1)
                    dve.wait_ge(pair_gated, part.count(2, q))
                    nc.vector.tensor_copy(act_hi[:, slot, part.cols], src).then_inc(pair_hi, 1)
                    dve.wait_ge(pair_hi, part.count(2, q))
                nc.vector.tensor_tensor(act_lo[:, slot, part.cols], src, act_hi[:, slot, part.cols].bitcast(F32),
                                        ALU.subtract).then_inc(signal, 1)

            def logits(part):
                ts = part.ts
                dve.wait_ge(logits_mm, part.count(1, 0))
                nc.vector.tensor_tensor(gl[:, ts], gate_ps(part)[:, :, 0],
                                        bbc[:, 0:NEXP].unsqueeze(1).to_broadcast([P, part.width, NEXP]),
                                        ALU.add).then_inc(logits_step, 1)
                dve.wait_ge(logits_step, part.count(2, 0))
                nc.vector.tensor_tensor(gl[:, ts], gate_ps(part)[:, :, 1], gl[:, ts], ALU.add
                                        ).then_inc(logits_step, 1)

            def gate(part):
                dve.wait_ge(logits_step, part.count(2, 1))
                softmax_argument(part)

            def softmax_argument(part):
                ts = part.ts
                nc.vector.tensor_reduce(gm[:, 0, ts], gl[:, ts], AX_X, ALU.max).then_inc(gate_step, 1)
                dve.wait_ge(gate_step, part.count(GATE_STEPS, 0))
                nc.vector.tensor_tensor(gd[:, ts], gl[:, ts], spread(gm[:, 0], part), ALU.subtract
                                        ).then_inc(gate_step, 1)

            def softmax(part):
                ts = part.ts
                step = lambda k: part.count(GATE_STEPS, 1 + k)
                dve.wait_ge(gate_exp, part.count(2, 0))
                nc.vector.tensor_reduce(gm[:, 1, ts], ge[:, ts], AX_X, ALU.add).then_inc(gate_step, 1)
                dve.wait_ge(gate_step, step(1))
                nc.vector.reciprocal(gm[:, 2, ts], gm[:, 1, ts]).then_inc(gate_step, 1)
                dve.wait_ge(gate_step, step(2))
                nc.vector.tensor_tensor(gates[:, ts], ge[:, ts], spread(gm[:, 2], part), ALU.mult
                                        ).then_inc(gate_step, 1)
                dve.wait_ge(gate_step, step(3))
                nc.vector.tensor_reduce(gm[:, 3, ts], gates[:, ts], AX_X, ALU.max).then_inc(gate_step, 1)
                dve.wait_ge(gate_step, step(4))
                nc.vector.tensor_tensor(gd[:, ts], gates[:, ts], spread(gm[:, 3], part), ALU.subtract
                                        ).then_inc(gate_step, 1)

            def top2(part):
                ts, w = part.ts, part.width
                step = lambda k: part.count(GATE_STEPS, 6 + k)
                mine = gates[:, ts].unsqueeze(3).to_broadcast([P, w, NEXP, NEXP])
                other = gates[:, ts].unsqueeze(2).to_broadcast([P, w, NEXP, NEXP])
                lower = cst[:, C_LOWER:C_LOWER + NEXP * NEXP].rearrange("p (e j) -> p e j", e=NEXP)
                nc.vector.tensor_tensor(ties[:, ts], other, mine, ALU.is_equal).then_inc(gate_step, 1)
                nc.vector.tensor_tensor(beats[:, ts], other, mine, ALU.is_gt).then_inc(gate_step, 1)
                dve.wait_ge(gate_step, step(2))
                nc.vector.tensor_tensor(ties[:, ts], ties[:, ts],
                                        lower.unsqueeze(1).to_broadcast([P, w, NEXP, NEXP]),
                                        ALU.mult).then_inc(gate_step, 1)
                dve.wait_ge(gate_step, step(3))
                nc.vector.tensor_tensor(beats[:, ts], beats[:, ts], ties[:, ts], ALU.add).then_inc(gate_step, 1)
                dve.wait_ge(gate_step, step(4))
                nc.vector.tensor_reduce(rank[:, ts], beats[:, ts], AX_X, ALU.add).then_inc(gate_step, 1)
                dve.wait_ge(gate_step, step(5))
                dve.wait_ge(gate_exp, part.count(2, 1))
                nc.vector.scalar_tensor_tensor(out=gw[:, ts], in0=rank[:, ts], scalar=float(TOPK) - 0.5,
                                               in1=ge[:, ts], op0=ALU.is_lt, op1=ALU.mult).then_inc(gate_step, 1)
                dve.wait_ge(gate_step, step(6))
                nc.vector.tensor_reduce(gm[:, 1, ts], gw[:, ts], AX_X, ALU.add).then_inc(gate_step, 1)
                dve.wait_ge(gate_step, step(7))
                nc.vector.reciprocal(gm[:, 2, ts], gm[:, 1, ts]).then_inc(gate_step, 1)
                dve.wait_ge(gate_step, step(8))
                nc.vector.tensor_tensor(gw[:, ts], gw[:, ts], spread(gm[:, 2], part), ALU.mult
                                        ).then_inc(gate_step, 1)
                dve.wait_ge(gate_step, step(9))
                nc.vector.tensor_copy(gw_hi[:, ts], gw[:, ts]).then_inc(gate_step, 1)
                dve.wait_ge(gate_step, step(10))
                for k in range(2):
                    nc.vector.tensor_copy(w_ext[:, ts, k * NEXP:(k + 1) * NEXP], gw_hi[:, ts].bitcast(F32))
                nc.vector.tensor_tensor(w_ext[:, ts, 2 * NEXP:3 * NEXP], gw[:, ts], gw_hi[:, ts].bitcast(F32),
                                        ALU.subtract).then_inc(gate_ready, 1)

            def result(part):
                dve.wait_ge(out_mm, part.count(1, 0))
                dve.wait_ge(y_free, part.n + 1)
                nc.vector.scalar_tensor_tensor(out=y[:, part.cols], in0=ps(part, OUT_BANK),
                                               scalar=bcol[:, B_OUT:B_OUT + 1], in1=x1[:, part.cols],
                                               op0=ALU.add, op1=ALU.add).then_inc(out_ready, 1)

            def stage(part, name, k):
                if name == "conv":
                    conv(part, k)
                if name == "merge":
                    merge(part)
                if name == "tokens":
                    tokens(part)
                if name == "normalise":
                    normalise_x1(part)
                if name == "features":
                    features(part)
                if name == "logits":
                    logits(part)
                if name == "gate":
                    gate(part)
                if name == "softmax":
                    softmax(part)
                if name == "top2":
                    top2(part)
                if name == "mlp":
                    mlp(part, k)
                if name == "out":
                    result(part)

            def setup():
                dve.wait_ge(const_landed, 80)
                nc.vector.tensor_scalar(scale[:], bbc[:, NEXP:NEXP + 2], 1.0, 1.0, ALU.add, ALU.add
                                        ).then_inc(dve_setup, 1)
                nc.vector.tensor_copy(brow_hi[:], brow[:]).then_inc(setup_step, 1)
                dve.wait_ge(setup_step, 1)
                nc.vector.tensor_tensor(brow_lo[:], brow[:], brow_hi[:].bitcast(F32), ALU.subtract
                                        ).then_inc(setup_step, 1)
                dve.wait_ge(setup_step, 2)
                nc.vector.tensor_scalar(brow_lo[:], brow_lo[:], cst[0:WROWS, C_PART + 1:C_PART + 2], None, ALU.mult
                                        ).then_inc(setup_step, 1)
                dve.wait_ge(setup_step, 3)
                nc.vector.scalar_tensor_tensor(out=brow_ext[:], in0=brow_hi[:].bitcast(F32),
                                               scalar=cst[0:WROWS, C_PART:C_PART + 1], in1=brow_lo[:],
                                               op0=ALU.mult, op1=ALU.add).then_inc(dve_setup, 1)

            nc.vector.memset(warm[:], 0.0).then_inc(warm_ready, 1)
            moments_x(0)
            for c in range(CHUNKS):
                g = c // 2
                if c % 2 == 0:
                    split_chunk(0, c)
                    normalise(g + 1, g % 2, work[:, nth["x"][g] % PIECE_RING, :], ztmp[:, g % 2, :], range(T))
                else:
                    split_chunk(0, c)
                    split_z(g)
                    if g + 1 < XG:
                        moments_x(g + 1)
                if c == CHUNKS // 2 + 1:
                    setup()
            with dve.Fori(1, NB) as b:
                for c in range(CHUNKS + LEAD):
                    if c < CHUNKS:
                        split_chunk(b, c)
                    if c == LEAD - 1:
                        aggregated(b - 1)
                    for name, k, at in STAGES:
                        if at == c - LEAD:
                            stage(Part(b - 1), name, k)
            def last_conv_input(part, _):
                dve.wait_ge(adj_used, NB * CHUNKS)
                nc.vector.tensor_scalar(work[:, 5, part.cols], agg[1][:, part.cols], scale[:, 1:2], None, ALU.mult
                                        ).then_inc(last_conv_in[1][part.half], 1)

            def last_conv(part, s):
                dve.wait_ge(last_conv_mm[1][part.half], s + 1)
                nc.vector.tensor_scalar(work[:, 5, part.cols], last_ps(LAST_CONV[1], part),
                                        bcol[:, LAYERS + s:LAYERS + s + 1], 0.0, ALU.add, ALU.max
                                        ).then_inc(last_conv_in[1][part.half], 1)

            def last_merge(part, _):
                dve.wait_ge(last_merge_mm[part.half], 1)
                dve.wait_ge(xres_landed, NB * 16)
                nc.vector.scalar_tensor_tensor(out=x1[:, part.cols], in0=last_ps(LAST_MERGE, part),
                                               scalar=bcol[:, B_MERGE:B_MERGE + 1], in1=xres[:, part.cols],
                                               op0=ALU.add, op1=ALU.add).then_inc(last_x1[part.half], 1)

            def last_bank(which, part):
                return banks[:, LAST_BANKS[part.half]["WXYZ".index(which)], :]

            def last_tokens(part, _):
                dve.wait_ge(last_tokens_mm[part.half], 1)
                bank = last_bank(LAST_TOKENS, part)
                nc.vector.tensor_copy(waiter[:, 1:2], bank[:, part.cols.start:part.cols.start + 1])
                moments(part.norm + XG, 0, bank, part.tiles)

            def last_normalise(part, _):
                normalise(part.norm + XG, 0, last_bank(LAST_TOKENS, part), ln_x1, part.tiles)

            def last_logit(part, _):
                dve.wait_ge(last_logits_mm[part.half], 1)
                nc.vector.tensor_tensor(gl[:, part.ts], last_gate_ps(part)[:, :, 0],
                                        bbc[:, 0:NEXP].unsqueeze(1).to_broadcast([P, part.width, NEXP]),
                                        ALU.add).then_inc(last_logits[part.half], 1)
                dve.wait_ge(last_logits[part.half], 1)
                nc.vector.tensor_tensor(gl[:, part.ts], last_gate_ps(part)[:, :, 1], gl[:, part.ts], ALU.add
                                        ).then_inc(last_logits[part.half], 1)

            def last_gate(part, _):
                for h in range(2):
                    dve.wait_ge(last_logits[h], 2)
                softmax_argument(part)

            def last_features(part, _):
                dve.wait_ge(last_lnT_hi[part.half], 1)
                nc.vector.tensor_tensor(act_lo[:, 3, part.cols], last_ps(LAST_FEATURES, part),
                                        act_hi[:, 3, part.cols].bitcast(F32), ALU.subtract
                                        ).then_inc(last_lnT_lo[part.half], 1)

            def last_pair(part, q):
                dve.wait_ge(last_mlp_h[part.half], 7 + q)
                dve.wait_ge(last_spread_mm, q + 1)
                src = work[:, 5 + q, part.cols]
                nc.vector.tensor_tensor(src, src, banks[:, last_spread_bank[q], part.cols], ALU.mult
                                        ).then_inc(last_gated[part.half], 1)

            def last_result(part, _):
                dve.wait_ge(last_out_mm[part.half], 1)
                dve.wait_ge(y_free, NB)
                nc.vector.scalar_tensor_tensor(out=y[:, part.cols], in0=banks[:, last_out_bank[part.half], part.cols],
                                               scalar=bcol[:, B_OUT:B_OUT + 1], in1=x1[:, part.cols],
                                               op0=ALU.add, op1=ALU.add).then_inc(last_out[part.half], 1)

            last_stages({"input": last_conv_input, "conv": last_conv, "merge": last_merge, "tokens": last_tokens,
                         "normalise": last_normalise, "logits": last_logit, "gate": last_gate,
                         "features": last_features, "softmax": lambda part, _: softmax(part),
                         "top2": lambda part, _: top2(part), "pair": last_pair,
                         "out": last_result})

        @block.tensor
        def _(pe):
            def hi_passes(dst, k, xh, start):
                nc.tensor.matmul(dst, wtile(w_hi, k), xh, start=start, stop=False)
                nc.tensor.matmul(dst, wtile(w_lo, k), xh, start=False, stop=False)

            def lo_pass(dst, k, xl, stop):
                return nc.tensor.matmul(dst, wtile(w_hi, k), xl, start=False, stop=stop)

            def aggregate(b, c, v):
                pe.wait_ge(adj_lo_ready, b * CHUNKS + (c + 1))
                if c == 0 and not peeled(b):
                    pe.wait_ge(agg_lo, b * 2 + (v - 1))
                for k in range(CW):
                    zh = z_hi[:, CW * c + k, v * P:(v + 1) * P]
                    zl = z_lo[:, CW * c + k, v * P:(v + 1) * P]
                    ah = adj_hi[:, c % SPLIT_RING, k * ROWS:(k + 1) * ROWS]
                    al = adj_lo[:, c % SPLIT_RING, k * ROWS:(k + 1) * ROWS]
                    nc.tensor.matmul(agg[v], zh, ah, start=(c == 0 and k == 0), stop=False)
                    nc.tensor.matmul(agg[v], zl, ah, start=False, stop=False)
                    ins = nc.tensor.matmul(agg[v], zh, al, start=False, stop=(c == CHUNKS - 1 and k == CW - 1))
                return ins

            def conv(part, s):
                for v in range(2):
                    k, dst = LAYERS * v + s, ps(part, CONV_BANK[s][v])
                    if s == 0:
                        pe.wait_ge(agg_lo, part.n * 2 + (v + 1))
                    else:
                        pe.wait_ge(conv_hi, part.count(6, 2 * s - 2, v))
                    hi_passes(dst, k, act_hi[:, v, part.cols], True)
                    if s > 0:
                        pe.wait_ge(conv_lo, part.count(6, 2 * s - 2, v))
                    lo_pass(dst, k, act_lo[:, v, part.cols], True).then_inc(conv_mm, 1)

            def merge(part):
                dst = ps(part, MERGE_BANK)
                for v in range(2):
                    pe.wait_ge(conv_hi, part.count(6, 4, v))
                    hi_passes(dst, W_MERGE + v, act_hi[:, v, part.cols], v == 0)
                    pe.wait_ge(conv_lo, part.count(6, 4, v))
                    ins = lo_pass(dst, W_MERGE + v, act_lo[:, v, part.cols], v == 1)
                ins.then_inc(merge_mm, 1)

            def tokens(part):
                pe.wait_ge(x1_ready, part.count(1, 0))
                bank = ps(part, TOKENS_BANK)
                for t in part.tiles:
                    ins = nc.tensor.transpose(bank[:, tile_cols(t)], x1[:, tile_cols(t)], cst[:, C_ID:C_ID + P])
                ins.then_inc(tokens_mm, 1)

            def features(part):
                pe.wait_ge(ln_done, part.norm + XG)
                bank = ps(part, FEATURES_BANK)
                for t in part.tiles:
                    ins = nc.tensor.transpose(bank[:, tile_cols(t)], ln_x1[:, tile_cols(t)], cst[:, C_ID:C_ID + P])
                ins.then_inc(lnT_mm, 1)

            def logits(part):
                pe.wait_ge(lnT_hi, part.count(1, 0))
                pe.wait_ge(lnT_lo, part.count(1, 0))
                gate_products(part, gate_ps(part)).then_inc(logits_mm, 1)

            def gate_products(part, sums):
                for i, t in enumerate(part.tiles):
                    dst = sums[:, i].rearrange("p k e -> p (k e)")
                    nc.tensor.matmul(dst, act_hi[:, 3, tile_cols(t)], w_gate[:], start=True, stop=False,
                                     skip_group_check=True)
                    ins = nc.tensor.matmul(dst[:, 0:NEXP], act_lo[:, 3, tile_cols(t)], w_gate[:, 0:NEXP],
                                           start=False, stop=True, skip_group_check=True)
                return ins

            def mlp(part, j):
                dst = ps(part, MLP_BANK[j])
                if j == 3:
                    pe.wait_ge(logits_step, part.count(2, 1))
                if j == 4:
                    pe.wait_ge(mlp_h, part.count(8, 0))
                if j <= NEXP:
                    k = W_SHARED if j == 0 else W_EXP1 + j - 1
                    hi_passes(dst, k, act_hi[:, 3, part.cols], True)
                    lo_pass(dst, k, act_lo[:, 3, part.cols], True).then_inc(mlp_mm, 1)
                elif j == 5:
                    pe.wait_ge(mlp_h, part.count(8, 1))
                    pe.wait_ge(shared_lo, part.count(2, 0))
                    hi_passes(dst, W_SHARED + 1, act_hi[:, 0, part.cols], True)
                    lo_pass(dst, W_SHARED + 1, act_lo[:, 0, part.cols], True).then_inc(mlp_mm, 1)
                else:
                    q = j - 6
                    pe.wait_ge(mlp_h, part.count(8, 2 * q + 2))
                    for i in range(2):
                        e = 2 * q + i
                        ins = nc.tensor.matmul(dst[i * EH:(i + 1) * EH], w_exp2[:, e * EH:(e + 1) * EH],
                                               work[:, e, part.cols], start=True, stop=True)
                    ins.then_inc(mlp_mm, 1)

            def rows(part):
                pe.wait_ge(mlp_h, part.count(8, 3))
                pe.wait_ge(gate_ready, part.count(1, 0))
                bank = ps(part, ROWS_BANK)
                for t in part.tiles:
                    ins = nc.tensor.transpose(bank[0:WROWS, tile_cols(t)], w_ext[:, t, :], cst[:, C_ID:C_ID + P])
                ins.then_inc(wT_mm, 1)

            def spread_weights(part):
                pe.wait_ge(wT_ready, part.count(1, 0))
                for q in range(2):
                    if q == 1:
                        pe.wait_ge(mlp_h, part.count(8, 5))
                    nc.tensor.matmul(spread_ps(part, q), sel[:, tile_cols(q)], wT[:, part.cols],
                                     start=True, stop=True).then_inc(spread_mm, 1)

            def output(part):
                dst = ps(part, OUT_BANK)
                pe.wait_ge(shared_lo, part.count(2, 1))
                pe.wait_ge(mlp_h, part.count(8, 6))
                nc.tensor.matmul(dst, brow_ext[:], wT[:, part.cols], start=True, stop=False)
                hi_passes(dst, W_SHARED + 2, act_hi[:, 0, part.cols], False)
                lo_pass(dst, W_SHARED + 2, act_lo[:, 0, part.cols], False)
                for q in range(2):
                    pe.wait_ge(pair_hi, part.count(2, q))
                    hi_passes(dst, W_EXP3 + q, act_hi[:, 1 + q, part.cols], False)
                    pe.wait_ge(pair_lo, part.count(2, q))
                    ins = lo_pass(dst, W_EXP3 + q, act_lo[:, 1 + q, part.cols], q == 1)
                ins.then_inc(out_mm, 1)

            def stage(part, name, k):
                if name == "conv":
                    conv(part, k)
                if name == "merge":
                    merge(part)
                if name == "tokens":
                    tokens(part)
                if name == "features":
                    features(part)
                if name == "logits":
                    logits(part)
                if name == "mlp":
                    mlp(part, k)
                if name == "rows":
                    rows(part)
                if name == "spread":
                    spread_weights(part)
                if name == "out":
                    output(part)

            for g in range(XG):
                first, second = 2 * g, 2 * g + 1
                if g < XG - 1:
                    passes = ((first, 1), (second, 1), (first, 0), (second, 0))
                else:
                    passes = ((first, 1), (first, 0), (second, 0), (second, 1))
                for i, (c, v) in enumerate(passes):
                    if i == 0:
                        pe.wait_ge(x2_lo, g + 1)
                    if (c, v) == (first, 0):
                        pe.wait_ge(z_lo_ready, g + 1)
                    ins = aggregate(0, c, v)
                    if (c, v) == (CHUNKS - 1, 0):
                        ins.then_inc(agg_half_done, 1)
                    elif c not in [later for later, _ in passes[i + 1:]]:
                        ins.then_inc(adj_used, 1)
            pe.wait_ge(w_lo_ready, WPIECES)
            pe.wait_ge(act_setup, 3)
            pe.wait_ge(dve_setup, 2)
            with pe.Fori(1, NB) as b:
                for c, v, step in PASSES:
                    ins = aggregate(b, c, v)
                    if v == 1:
                        ins.then_inc(adj_used, 1)
                    elif c == CHUNKS - 1:
                        ins.then_inc(agg_half_done, 1)
                    for name, k, at in STAGES:
                        if at == step:
                            stage(Part(b - 1), name, k)
            def plain(dst, k, rhs, start=True, stop=True):
                return nc.tensor.matmul(dst, wtile(w_plain, k), rhs, start=start, stop=stop)

            def last_conv(part, s):
                for v in range(2):
                    pe.wait_ge(last_conv_in[v][part.half], s + 1)
                    plain(last_ps(LAST_CONV[v], part), LAYERS * v + s, work[:, 4 + v, part.cols]
                          ).then_inc(last_conv_mm[v][part.half], 1)

            def last_merge(part, _):
                for v in range(2):
                    pe.wait_ge(last_conv_in[v][part.half], LAYERS + 1)
                    ins = plain(last_ps(LAST_MERGE, part), W_MERGE + v, work[:, 4 + v, part.cols], v == 0, v == 1)
                ins.then_inc(last_merge_mm[part.half], 1)

            def last_transposes(which, src, part):
                for t in part.tiles:
                    dst = last_ps(which, part)[:, tile_cols(t - part.tiles[0])]
                    ins = nc.tensor.transpose(dst, src[:, tile_cols(t)], cst[:, C_ID:C_ID + P])
                return ins

            def last_tokens(part, _):
                pe.wait_ge(last_x1[part.half], 1)
                last_transposes(LAST_TOKENS, x1, part).then_inc(last_tokens_mm[part.half], 1)

            def last_features(part, _):
                pe.wait_ge(ln_done, part.norm + XG)
                last_transposes(LAST_FEATURES, ln_x1, part).then_inc(last_lnT_mm[part.half], 1)

            def last_logit(part, _):
                pe.wait_ge(last_lnT_hi[part.half], 1)
                pe.wait_ge(last_lnT_lo[part.half], 1)
                gate_products(part, last_gate_ps(part)).then_inc(last_logits_mm[part.half], 1)

            def last_mlp(part, j):
                dst = last_ps(LAST_MLP[j], part)
                if j == 3:
                    pe.wait_ge(last_logits[part.half], 2)
                needed = {4: 1, 5: 2, 6: 3, 7: 5}
                if j in needed:
                    pe.wait_ge(last_mlp_h[part.half], needed[j])
                if j <= NEXP:
                    k = W_SHARED if j == 0 else W_EXP1 + j - 1
                    hi_passes(dst, k, act_hi[:, 3, part.cols], True)
                    ins = lo_pass(dst, k, act_lo[:, 3, part.cols], True)
                elif j == 5:
                    ins = plain(dst, W_SHARED + 1, work[:, 4, part.cols])
                else:
                    for i in range(2):
                        e = 2 * (j - 6) + i
                        ins = nc.tensor.matmul(dst[i * EH:(i + 1) * EH], w_exp2[:, e * EH:(e + 1) * EH],
                                               work[:, e, part.cols], start=True, stop=True)
                ins.then_inc(last_mlp_mm[part.half], 1)

            def last_gate_rows(part, _):
                pe.wait_ge(gate_ready, NB)
                pe.wait_ge(last_mlp_h[0], 5)
                for t in part.tiles:
                    ins = nc.tensor.transpose(banks[0:WROWS, last_rows_bank, tile_cols(t)], w_ext[:, t, :],
                                              cst[:, C_ID:C_ID + P])
                ins.then_inc(last_rows_mm, 1)

            def last_spread(part, _):
                pe.wait_ge(last_rows, 1)
                for q, (h, done) in enumerate(((1, 5), (0, 6))):
                    pe.wait_ge(last_mlp_h[h], done)
                    nc.tensor.matmul(banks[:, last_spread_bank[q], :], sel[:, tile_cols(q)], wT[:],
                                     start=True, stop=True).then_inc(last_spread_mm, 1)

            def last_output(part, _):
                pe.wait_ge(last_mlp_h[part.half], 6)
                dst = banks[:, last_out_bank[part.half], part.cols]
                nc.tensor.matmul(dst, brow_ext[:], wT[:, part.cols], start=True, stop=False)
                plain(dst, W_SHARED + 2, work[:, 4, part.cols], False, False)
                for q in range(2):
                    pe.wait_ge(last_gated[part.half], q + 1)
                    ins = plain(dst, W_EXP3 + q, work[:, 5 + q, part.cols], False, q == 1)
                ins.then_inc(last_out_mm[part.half], 1)

            def keep_warm(_, times):
                for k in range(times):
                    nc.tensor.matmul(banks[:, LAST_BANKS[0][0], :], z_hi[:, 0, 0:P], adj_hi[:, 0, 0:ROWS],
                                     start=True, stop=True, skip_group_check=True)

            pe.wait_ge(last_weights, 16)
            last_stages({"conv": last_conv, "merge": last_merge, "tokens": last_tokens,
                         "features": last_features, "logits": last_logit, "mlp": last_mlp,
                         "warm": keep_warm, "rows": last_gate_rows, "spread": last_spread, "out": last_output})


def _layout(a):
    import numpy as np

    n = a["adj"].shape[0]
    nb = n // ROWS
    adj = a["adj"].reshape(nb, P, T, nb, P, T).transpose(0, 4, 3, 5, 2, 1).reshape(nb * P, n * T)

    eW3 = a["L0_ffn_eW3"]
    weights = np.concatenate(
        [a["L0_gnn_W1"][k].T for k in range(LAYERS)] + [a["L0_gnn_W2"][k].T for k in range(LAYERS)]
        + [a["L0_gnn_Wm"][:, :P].T, a["L0_gnn_Wm"][:, P:].T]
        + [a["L0_ffn_sW1"], a["L0_ffn_sW2"], a["L0_ffn_sW3"]]
        + [a["L0_ffn_eW1"][e] for e in range(NEXP)]
        + [eW3[2 * q:2 * q + 2].reshape(P, P) for q in range(NEXP // 2)] + [a["L0_ffn_gW"]], axis=1)
    bias_cols = np.concatenate([a["L0_gnn_b1"], a["L0_gnn_b2"], a["L0_ffn_sb1"][None], a["L0_ffn_sb2"][None],
                                a["L0_ffn_eb1"], a["L0_ffn_eb2"].reshape(NEXP // 2, P),
                                a["L0_gnn_bm"][None], a["L0_ffn_sb3"][None]]).T
    bias_bc = np.concatenate([a["L0_ffn_gb"], a["L0_gnn_eps1"], a["L0_gnn_eps2"]])
    bias_rows = np.concatenate([a["L0_ffn_eb3"]] * 3)

    consts = np.zeros((P, C_COLS), np.float32)
    consts[:, C_ID:C_ID + P] = np.eye(P)
    for e in range(NEXP):
        for row in (e, 2 * NEXP + e):
            consts[row, C_SEL + 64 * e:C_SEL + 64 * (e + 1)] = 1
    consts[:, C_LOWER:C_PART] = np.tril(np.ones((NEXP, NEXP)), -1).reshape(-1)
    hi_rows = np.array([1] * NEXP + [0] * NEXP + [1] * NEXP)
    consts[:WROWS, C_PART] = hi_rows
    consts[:WROWS, C_PART + 1] = 1 - hi_rows
    xT = a["x"].reshape(nb, P, T, P).transpose(3, 0, 2, 1).reshape(P, n)
    return {"adj": adj, "x": a["x"], "xT": xT, "x2": a["L0_gnn_x2"], "weights": weights,
            "w_exp2": a["L0_ffn_eW2"].transpose(1, 0, 2).reshape(P, NEXP * EH), "bias_cols": bias_cols,
            "bias_bc": bias_bc, "bias_rows": bias_rows, "consts": consts}


def kernel(**inputs):
    import numpy as _np
    import concourse.bacc as _bacc
    from concourse import mybir as _mybir
    from concourse.bass_utils import run_bass_kernel_spmd as _run

    nc = _bacc.Bacc("TRN2", target_bir_lowering=False, num_devices=1)
    arrays, args = {}, []
    for name, a in _layout({k: _np.asarray(v) for k, v in inputs.items()}).items():
        a = _np.ascontiguousarray(a)
        arrays[f"in_{name}_dram"] = a
        args.append(nc.dram_tensor(f"in_{name}_dram", a.shape, _mybir.dt.from_np(a.dtype), kind="ExternalInput").ap())
    rows, width = inputs["x"].shape
    args.append(nc.dram_tensor("out_0_dram", (width, rows), _mybir.dt.float32, kind="ExternalOutput").ap())
    gnn_moe_kernel(nc, *args)
    r = _run(nc, [arrays], core_ids=[0])
    got = r.results[0]["out_0_dram"].reshape(width, rows // ROWS, T, P)
    return _np.ascontiguousarray(got.transpose(1, 3, 2, 0).reshape(rows, width))
```
